# Optimizing a Trainium2 kernel written in Bass

```python
import numpy as np
import jax
import jax.numpy as jnp

def _softmax(x, axis=-1):
    return jax.nn.softmax(x, axis=axis)

def _gelu(x):
    return jax.nn.gelu(x, approximate=True)

def _silu(x):
    return jax.nn.silu(x)

def _sigmoid(x):
    return jax.nn.sigmoid(x)

def _layernorm(x, axis=-1, eps=1e-05):
    m = jnp.mean(x, axis=axis, keepdims=True)
    v = jnp.var(x, axis=axis, keepdims=True)
    return (x - m) / jnp.sqrt(v + eps)

def _scatter_add(tgt, idx, src, axis=0):
    return tgt.at[idx].add(src)

def _segment_sum(src, seg, n):
    return jax.ops.segment_sum(src, seg, n)
kernel_name = 'mk_gnn_resnorm_d4_gnn_r32_7a429c'

def setup_inputs(seed: int=0):
    np.random.seed(seed)
    _w = jnp.asarray

    def _rec_inputs():
        import jax
        import jax.numpy as jnp
        _gk = jax.random.key(seed)
        x = -0.001812 + 1 * jax.random.normal(jax.random.fold_in(_gk, 1), (3125, 16), jnp.float32)
        src = jax.random.randint(jax.random.fold_in(_gk, 2), (100000,), 0, 3125, jnp.int32)
        dst = jnp.minimum((3125 * jax.random.uniform(jax.random.fold_in(_gk, 3), (100000,)) ** 2.0).astype(jnp.int32), 99999)
        _o = jnp.argsort(dst, stable=True)
        src = src[_o]
        dst = dst[_o]
        edge_attr_16 = 0.000268479 + 0.999861 * jax.random.normal(jax.random.fold_in(_gk, 12), (100000, 16), jnp.float32)
        return (x, src, dst, edge_attr_16)
    x, src, dst, edge_attr_16 = _rec_inputs()

    def _L0_gnn_setup():
        import jax, jax.numpy as jnp
        import numpy as np
        N_NODES = 625
        N_EDGES = 20000
        F = 16

        def _nnconv(x, src, dst, edge_attr, Wn, bn, Wr, b, n_nodes):
            E = edge_attr.shape[0]
            f_in = x.shape[-1]
            f_out = Wr.shape[-1]
            w = jax.nn.relu(edge_attr @ Wn + bn).reshape(E, f_in, f_out)
            msg = jnp.einsum('ei,eio->eo', x[src], w)
            sums = jax.ops.segment_sum(msg, dst, num_segments=n_nodes)
            cnt = jax.ops.segment_sum(jnp.ones((E,), dtype=x.dtype), dst, num_segments=n_nodes)
            aggr = sums / jnp.maximum(cnt, 1.0)[:, None]
            return aggr + x @ Wr + b
        key = jax.random.key(seed)
        ks = jax.random.split(key, 12)
        s_nn = 1.0 / np.sqrt(F)
        s_r = 1.0 / np.sqrt(F)
        inp = {'x': jax.random.normal(ks[0], (N_NODES, F), dtype=jnp.float32), 'edge_index': jax.random.randint(ks[1], (2, N_EDGES), 0, N_NODES, dtype=jnp.int32), 'edge_attr': jax.random.normal(ks[2], (N_EDGES, F), dtype=jnp.float32)}
        for l, (kw, kr) in enumerate(zip(ks[3:6], ks[6:9]), start=1):
            inp[f'Wn{l}'] = jax.random.normal(kw, (F, F * F), dtype=jnp.float32) * s_nn
            inp[f'bn{l}'] = jnp.zeros((F * F,), dtype=jnp.float32)
            inp[f'Wr{l}'] = jax.random.normal(kr, (F, F), dtype=jnp.float32) * s_r
            inp[f'b{l}'] = jnp.zeros((F,), dtype=jnp.float32)
        return inp
    _L0_gnn_all = _L0_gnn_setup()
    _L0_gnn_in = {k: v for k, v in _L0_gnn_all.items() if k in ('Wn1', 'bn1', 'Wr1', 'b1', 'Wn2', 'bn2', 'Wr2', 'b2', 'Wn3', 'bn3', 'Wr3', 'b3')}
    del _L0_gnn_all

    def _L1_gnn_setup():
        import jax, jax.numpy as jnp
        import numpy as np
        N_NODES = 3125
        N_EDGES = 15625
        IND = 16
        OUT = 16
        EDGE_DIM = 16
        HID = IND * OUT
        BN_EPS = 1e-05
        key = jax.random.key(seed)
        ks = jax.random.split(key, 12)
        x = jax.random.normal(ks[0], (N_NODES, IND), dtype=jnp.float32)
        edge_index = jax.random.randint(ks[1], (2, N_EDGES), 0, N_NODES, dtype=jnp.int64)
        edge_attr = jax.random.normal(ks[2], (N_EDGES, EDGE_DIM), dtype=jnp.float32)
        W1 = jax.random.normal(ks[3], (EDGE_DIM, HID), dtype=jnp.float32) * (1.0 / np.sqrt(EDGE_DIM))
        b1 = jnp.zeros((HID,), dtype=jnp.float32)
        W2 = jax.random.normal(ks[4], (HID, HID), dtype=jnp.float32) * (1.0 / np.sqrt(HID))
        b2 = jnp.zeros((HID,), dtype=jnp.float32)
        root = jax.random.normal(ks[5], (IND, OUT), dtype=jnp.float32) * (1.0 / np.sqrt(IND))
        bias = jnp.zeros((OUT,), dtype=jnp.float32)
        gamma = jnp.ones((OUT,), dtype=jnp.float32)
        beta = jnp.zeros((OUT,), dtype=jnp.float32)
        return {'x': x, 'edge_index': edge_index, 'edge_attr': edge_attr, 'W1': W1, 'b1': b1, 'W2': W2, 'b2': b2, 'root': root, 'bias': bias, 'gamma': gamma, 'beta': beta}
    _L1_gnn_all = _L1_gnn_setup()
    _L1_gnn_in = {k: v for k, v in _L1_gnn_all.items() if k in ('W1', 'b1', 'W2', 'b2', 'root', 'bias', 'gamma', 'beta')}
    del _L1_gnn_all

    def _L2_gnn_setup():
        import jax, jax.numpy as jnp
        import numpy as np
        N_NODES = 3125
        N_EDGES = 100000
        D_FEAT = 16
        key = jax.random.key(seed)
        kx, ke = jax.random.split(key)
        x = jax.random.normal(kx, (N_NODES, D_FEAT), dtype=jnp.float32)
        edge_index = jax.random.randint(ke, (2, N_EDGES), 0, N_NODES, dtype=jnp.int64)
        return {'x': x, 'edge_index': edge_index}
    _L2_gnn_all = _L2_gnn_setup()
    _L2_gnn_in = {k: v for k, v in _L2_gnn_all.items() if k in ()}
    del _L2_gnn_all

    def _L3_gnn_setup():
        import jax, jax.numpy as jnp
        import numpy as np
        N_NODES = 3125
        key = jax.random.key(seed)
        k1, k2, k3 = jax.random.split(key, 3)
        features = jax.random.normal(k1, (N_NODES, 16), dtype=jnp.float32)
        src = jax.random.randint(k2, (156250,), 0, N_NODES, dtype=jnp.int64)
        dst = jax.random.randint(k3, (156250,), 0, N_NODES, dtype=jnp.int64)
        return {'features': features, 'src': src, 'dst': dst}
    _L3_gnn_all = _L3_gnn_setup()
    _L3_gnn_in = {k: v for k, v in _L3_gnn_all.items() if k in ()}
    del _L3_gnn_all
    return {'x': x, 'src': src, 'dst': dst, 'edge_attr_16': edge_attr_16, 'L0_gnn_Wn1': _L0_gnn_in['Wn1'], 'L0_gnn_bn1': _L0_gnn_in['bn1'], 'L0_gnn_Wr1': _L0_gnn_in['Wr1'], 'L0_gnn_b1': _L0_gnn_in['b1'], 'L0_gnn_Wn2': _L0_gnn_in['Wn2'], 'L0_gnn_bn2': _L0_gnn_in['bn2'], 'L0_gnn_Wr2': _L0_gnn_in['Wr2'], 'L0_gnn_b2': _L0_gnn_in['b2'], 'L0_gnn_Wn3': _L0_gnn_in['Wn3'], 'L0_gnn_bn3': _L0_gnn_in['bn3'], 'L0_gnn_Wr3': _L0_gnn_in['Wr3'], 'L0_gnn_b3': _L0_gnn_in['b3'], 'L1_gnn_W1': _L1_gnn_in['W1'], 'L1_gnn_b1': _L1_gnn_in['b1'], 'L1_gnn_W2': _L1_gnn_in['W2'], 'L1_gnn_b2': _L1_gnn_in['b2'], 'L1_gnn_root': _L1_gnn_in['root'], 'L1_gnn_bias': _L1_gnn_in['bias'], 'L1_gnn_gamma': _L1_gnn_in['gamma'], 'L1_gnn_beta': _L1_gnn_in['beta']}

def reference(x, src, dst, edge_attr_16, L0_gnn_Wn1, L0_gnn_bn1, L0_gnn_Wr1, L0_gnn_b1, L0_gnn_Wn2, L0_gnn_bn2, L0_gnn_Wr2, L0_gnn_b2, L0_gnn_Wn3, L0_gnn_bn3, L0_gnn_Wr3, L0_gnn_b3, L1_gnn_W1, L1_gnn_b1, L1_gnn_W2, L1_gnn_b2, L1_gnn_root, L1_gnn_bias, L1_gnn_gamma, L1_gnn_beta):
    import jax
    import jax.numpy as jnp

    def _L0_gnn_ref(x, edge_index, edge_attr, Wn1, bn1, Wr1, b1, Wn2, bn2, Wr2, b2, Wn3, bn3, Wr3, b3):
        import jax, jax.numpy as jnp
        import numpy as np
        N_NODES = 625
        N_EDGES = 20000
        F = 16

        def _nnconv(x, src, dst, edge_attr, Wn, bn, Wr, b, n_nodes):
            E = edge_attr.shape[0]
            f_in = x.shape[-1]
            f_out = Wr.shape[-1]
            w = jax.nn.relu(edge_attr @ Wn + bn).reshape(E, f_in, f_out)
            msg = jnp.einsum('ei,eio->eo', x[src], w)
            sums = jax.ops.segment_sum(msg, dst, num_segments=n_nodes)
            cnt = jax.ops.segment_sum(jnp.ones((E,), dtype=x.dtype), dst, num_segments=n_nodes)
            aggr = sums / jnp.maximum(cnt, 1.0)[:, None]
            return aggr + x @ Wr + b
        src, dst = (edge_index[0], edge_index[1])
        n = x.shape[0]
        h = _nnconv(x, src, dst, edge_attr, Wn1, bn1, Wr1, b1, n)
        h = _nnconv(h, src, dst, edge_attr, Wn2, bn2, Wr2, b2, n)
        h = _nnconv(h, src, dst, edge_attr, Wn3, bn3, Wr3, b3, n)
        return h

    def _L1_gnn_ref(x, edge_index, edge_attr, W1, b1, W2, b2, root, bias, gamma, beta):
        import jax, jax.numpy as jnp
        import numpy as np
        N_NODES = 3125
        N_EDGES = 15625
        IND = 16
        OUT = 16
        EDGE_DIM = 16
        HID = IND * OUT
        BN_EPS = 1e-05
        n_nodes, ind = x.shape
        out_dim = root.shape[1]
        src, dst = (edge_index[0], edge_index[1])
        h = jax.nn.relu(edge_attr @ W1 + b1)
        w_edge = (h @ W2 + b2).reshape(-1, ind, out_dim)
        msgs = jnp.einsum('ei,eio->eo', x[src], w_edge)
        aggr = jax.ops.segment_sum(msgs, dst, num_segments=n_nodes)
        out = aggr + x @ root + bias
        mean = out.mean(axis=0)
        var = out.var(axis=0)
        out = (out - mean) / jnp.sqrt(var + BN_EPS) * gamma + beta
        return jax.nn.relu(out)

    def _L2_gnn_ref(x, edge_index):
        import jax, jax.numpy as jnp
        import numpy as np
        N_NODES = 3125
        N_EDGES = 100000
        D_FEAT = 16
        row = edge_index[0]
        col = edge_index[1]
        msg = jnp.take(x, col, axis=0)
        tmp = jnp.take(msg, col, axis=0)
        out = jax.ops.segment_sum(tmp, row, num_segments=x.shape[0])
        return out

    def _L3_gnn_ref(features, src, dst):
        import jax, jax.numpy as jnp
        import numpy as np
        N_NODES = 3125
        n = features.shape[0]
        ones = jnp.ones(src.shape[0], dtype=features.dtype)
        out_deg = jnp.zeros(n, dtype=features.dtype).at[src].add(ones)
        out_deg = jnp.clip(out_deg, 1.0, None)
        in_deg = jnp.zeros(n, dtype=features.dtype).at[dst].add(ones)
        in_deg = jnp.clip(in_deg, 1.0, None)
        x = features * (out_deg ** (-0.5))[:, None]
        agg = jnp.zeros_like(features).at[dst].add(x[src])
        return agg * (in_deg ** (-0.5))[:, None]
    edge_index = jnp.stack([src, dst])
    x = _layernorm(x + _L0_gnn_ref(x, edge_index, edge_attr_16, L0_gnn_Wn1, L0_gnn_bn1, L0_gnn_Wr1, L0_gnn_b1, L0_gnn_Wn2, L0_gnn_bn2, L0_gnn_Wr2, L0_gnn_b2, L0_gnn_Wn3, L0_gnn_bn3, L0_gnn_Wr3, L0_gnn_b3), axis=-1)
    x = _layernorm(x + _L1_gnn_ref(x, edge_index, edge_attr_16, L1_gnn_W1, L1_gnn_b1, L1_gnn_W2, L1_gnn_b2, L1_gnn_root, L1_gnn_bias, L1_gnn_gamma, L1_gnn_beta), axis=-1)
    x = _layernorm(x + _L2_gnn_ref(x, edge_index), axis=-1)
    x = _layernorm(x + _L3_gnn_ref(x, src, dst), axis=-1)
    return x

_drawn_inputs = setup_inputs


def setup_inputs(seed=0):
    import zlib

    import numpy as np

    out = dict(_drawn_inputs(seed))
    spreads = {'L0_gnn_bn1': (0.0, 0.314),
     'L0_gnn_b1': (0.0, 0.1),
     'L0_gnn_bn2': (0.0, 0.1),
     'L0_gnn_b2': (0.0, 0.1),
     'L0_gnn_bn3': (0.0, 0.1),
     'L0_gnn_b3': (0.0, 0.1),
     'L1_gnn_b1': (0.0, 0.1),
     'L1_gnn_b2': (0.0, 0.1),
     'L1_gnn_bias': (0.0, 0.8),
     'L1_gnn_gamma': (1.0, 0.2),
     'L1_gnn_beta': (0.0, 0.8)}
    factors = {'L1_gnn_root': 8.0}
    for name, (base, spread) in spreads.items():
        noise = np.random.default_rng([zlib.crc32(name.encode()), seed]).standard_normal(out[name].shape)
        drawn = base * np.exp(spread * noise) if base else spread * noise
        out[name] = jnp.asarray(drawn.astype(out[name].dtype))
    for name, factor in factors.items():
        out[name] = (out[name] * factor).astype(out[name].dtype)
    return out
```

```python
import concourse.bass as bass
from concourse import mybir
from contextlib import ExitStack

N = 3125
E = 100000
F = 16
HID = F * F
P = 128
PIECES = 3
GT = 4
GE = GT * P
UN = 4
NG = -(-E // (GE * UN)) * UN
NT = NG * GT
EP = NT * P
IT = NG // UN
NB = -(-N // P)
NBT = NB + 1
NPAD = NBT * P
ACC = NB * F
STACK = (0, 0, 0, 1, 1, 2)
WSTACK = (0, 1, 2, 0, 1, 0)
KS = len(STACK) * F
EC = EP // 8
CH = 4
EW = EC // CH
LAST = N - (NB - 1) * P
EPS = 1e-5


def gnn_kernel(nc, x, srcT, dstT, eaT, wcat, bcol, rows, wroot, w2, consts, out):
    fp32, bf16, i32 = mybir.dt.float32, mybir.dt.bfloat16, mybir.dt.int32
    ALU, ACT, AX = mybir.AluOpType, mybir.ActivationFunctionType, mybir.AxisListType.X

    ctx = ExitStack()
    with ctx:
        def sb(name, shape, dt):
            return ctx.enter_context(nc.sbuf_tensor(name, shape, dt))

        def pb(name):
            return ctx.enter_context(nc.psum_tensor(name, [P, 512], fp32))

        def sem(name):
            return ctx.enter_context(nc.semaphore(name))

        stack_d = nc.dram_tensor("stack_d", [len(STACK) * P, EC], bf16).ap()
        parts_d = [nc.dram_tensor(f"parts_d{k}", [NPAD, PIECES * F], bf16).ap() for k in range(4)]
        rows_d = [nc.dram_tensor(f"rows_d{k}", [NPAD, F], fp32).ap() for k in range(3)]

        cst = sb("cst", [P, 5 * P + F + 8], fp32)
        ident = cst[:, 0:P]
        iota = cst[:, P:2 * P]
        live = cst[:, 2 * P:3 * P]
        sel = cst[:, 3 * P:3 * P + F]
        repf = cst[0:PIECES * F, 3 * P + F:5 * P + F]
        diag = cst[:, 5 * P + F:5 * P + F + 8]
        identb = sb("identb", [P, P], bf16)
        rep = sb("rep", [PIECES * F, 2 * P], bf16)
        ones = sb("ones", [P, P], fp32)
        wc = sb("wc", [F, 4 * HID], fp32)
        wpart = sb("wpart", [F, PIECES, 4 * HID], bf16)
        wstack = sb("wstack", [KS, 4 * HID], bf16)
        bc = sb("bc", [P, 10], fp32)
        row = sb("row", [P, 6, F], fp32)
        wrep = sb("wrep", [P, 4, F], fp32)
        wdiag = sb("wdiag", [P, 4, 8, F], fp32)
        w2s = sb("w2s", [P, 2, HID], fp32)

        src_i = sb("src_i", [P, NT + GT], i32)
        dst_i = sb("dst_i", [P, NT + GT], i32)
        tmp_i = sb("tmp_i", [P, NT], i32)
        src_a = sb("src_a", [P, NT], fp32)
        src_b = sb("src_b", [P, NT], fp32)
        dst_a = sb("dst_a", [P, NT], fp32)
        dst_b = sb("dst_b", [P, NT], fp32)

        ea_in = sb("ea_in", [P, 2, EW], fp32)
        ea_rest = sb("ea_rest", [P, 2, EW], fp32)
        ea_hi = sb("ea_hi", [P, 2, EW], bf16)
        ea_mid = sb("ea_mid", [P, 2, EW], bf16)
        ea_lo = sb("ea_lo", [P, 2, EW], bf16)

        ea_s = sb("ea_s", [KS, UN, GE], bf16)
        zero4 = sb("zero4", [P, GT], i32)
        stage = sb("stage", [P, UN * GT], i32)
        gp = sb("gp", [P, UN, GT, P], bf16)
        gf = sb("gf", [P, UN, GT, F], fp32)
        xts = sb("xts", [PIECES * F, 2, GE], bf16)
        relu = sb("relu", [P, 2, 2, GE], fp32)
        xrs = sb("xrs", [P, 2, 2, GE], fp32)
        prod = sb("prod", [P, 2, 2, GE], fp32)
        ohb = sb("ohb", [P, 2, GT, P], fp32)
        msk = sb("msk", [P, 2, GT, ACC + NB], fp32)

        X = sb("X", [P, NBT * F], fp32)
        X0 = sb("X0", [P, NBT * F], fp32)
        T48 = sb("T48", [P, NBT, PIECES * F], bf16)
        Rr = sb("Rr", [P, NBT * F], fp32)
        Y = sb("Y", [P, ACC], fp32)
        Z = sb("Z", [P, ACC], fp32)
        xnt = sb("xnt", [P, 512], fp32)
        cnt = sb("cnt", [P, 2, NB], fp32)
        icnt = sb("icnt", [P, NB], fp32)
        rdeg = sb("rdeg", [P, 2, NB], fp32)
        st1 = sb("st1", [P, NB], fp32)
        st2 = sb("st2", [P, NB], fp32)
        st3 = sb("st3", [P, NB], fp32)
        col = sb("col", [P, F], fp32)
        col2 = sb("col2", [P, F], fp32)
        col3 = sb("col3", [P, F], fp32)

        W = [pb("W0"), pb("W1")]
        XR = [pb("XR0"), pb("XR1")]
        TR = pb("TR")
        MS = [pb("MS0"), pb("MS1")]
        acc = pb("acc")
        xT = TR[:, 0:GE // 2].bitcast(bf16)

        def lin(ph, h):
            return W[0] if ph == 3 else W[h]

        V = [W[1], MS[1]]

        def msg(ph, r):
            return (MS[0] if ph == 3 else MS[r])[:, 0:GT * F]

        s_cst, s_x, s_idx, s_w, s_out = sem("s_cst"), sem("s_x"), sem("s_idx"), sem("s_wload"), sem("s_out")
        s_ein = [sem(f"s_ein{k}") for k in range(2)]
        s_est = [sem(f"s_est{k}") for k in range(2)]
        s_hi, s_rest, s_mid, s_lo = sem("s_hi"), sem("s_rest"), sem("s_mid"), sem("s_lo")
        s_wparts, s_wstack = sem("s_wparts"), sem("s_wstack")
        s_dve = sem("s_dve")
        s_const = sem("s_const")
        s_tabready, s_tab = sem("s_tabready"), sem("s_tab")
        s_ea = [sem(f"s_ea{k}") for k in range(UN)]
        s_stage, s_pz = sem("s_stage"), sem("s_pz")
        s_g = [sem(f"s_g{k}") for k in range(UN)]
        s_xt, s_xts, s_lin, s_relu, s_w2 = sem("s_xt"), sem("s_xts"), sem("s_lin"), sem("s_relu"), sem("s_w2")
        s_xrep, s_xrs, s_prod, s_msg = sem("s_xrep"), sem("s_xrs"), sem("s_prod"), sem("s_msg")
        s_msk, s_scat = sem("s_msk"), sem("s_scat")
        s_ntr, s_ntc, s_root = sem("s_ntr"), sem("s_ntc"), sem("s_root")
        s_bnin, s_bnout = sem("s_bnin"), sem("s_bnout")
        s_var, s_std = sem("s_var"), sem("s_std")
        s_ytab, s_ygat = sem("s_ytab"), sem("s_ygat")

        block = ctx.enter_context(nc.Block())

        def blocks(ap, a):
            return ap.rearrange("p (a f) -> p a f", f=F)[:, 0:a, :]

        @block.sync
        def _(sp):
            sp.dma_start(cst[:], consts).then_inc(s_cst, 16)
            sp.dma_start(X[:], x.rearrange("(a b) f -> b a f", b=P)).then_inc(s_x, 16)
            sp.dma_start(X0[:], x.rearrange("(a b) f -> b a f", b=P)).then_inc(s_x, 16)
            sp.dma_start(src_i[:, 0:NT], srcT).then_inc(s_idx, 16)
            sp.dma_start(dst_i[:, 0:NT], dstT).then_inc(s_idx, 16)
            sp.dma_start(wc[:], wcat).then_inc(s_w, 16)
            sp.dma_start(bc[:], bcol).then_inc(s_w, 16)
            sp.dma_start(row[:].rearrange("p k f -> p (k f)"), rows.to_broadcast([P, 6 * F])).then_inc(s_w, 16)
            sp.dma_start(w2s[:], w2.rearrange("(k p) n -> p k n", p=P)).then_inc(s_w, 16)
            for a in range(8):
                sp.dma_start(wrep[F * a:F * a + F, :, :], wroot).then_inc(s_w, 16)
            for c in range(2):
                sp.dma_start(ea_in[:, c, :], eaT[:, c * EW:(c + 1) * EW]).then_inc(s_ein[c], 16)
            sp.wait_ge(s_wparts, 1)
            for k, q in enumerate(WSTACK):
                sp.dma_start(wstack[F * k:F * k + F, :], wpart[:, q, :]).then_inc(s_wstack, 16)
            for c in range(CH):
                sp.wait_ge(s_hi, c + 1)
                sp.wait_ge(s_mid, c + 1)
                sp.wait_ge(s_lo, c + 1)
                for k, q in enumerate(STACK):
                    part = (ea_hi, ea_mid, ea_lo)[q]
                    sp.dma_start(stack_d[k * P:(k + 1) * P, c * EW:(c + 1) * EW], part[:, c % 2, :])\
                      .then_inc(s_est[c % 2], 16)
                if c + 2 < CH:
                    sp.dma_start(ea_in[:, c % 2, :], eaT[:, (c + 2) * EW:(c + 3) * EW])\
                      .then_inc(s_ein[c % 2], 16)
            for c in range(2):
                sp.wait_ge(s_est[c], 16 * (CH // 2) * len(STACK))

            edges = stack_d.rearrange("(r c) n -> r (c n)", c=8)

            def load(ph, i, first=False):
                for u in range(UN):
                    n = NG * ph + UN * i + u
                    if not first:
                        sp.wait_ge(s_lin, 2 * (n - UN) + 2)
                    sp.dma_start(ea_s[:, u, :], edges[:, bass.ds((UN * i + u) * GE, GE)])\
                      .then_inc(s_ea[u], 16)

            for ph in range(6):
                if ph < 4:
                    sp.wait_ge(s_tabready, ph + 1)
                    sp.dma_start(parts_d[ph].rearrange("(a b) f -> b a f", b=P), T48[:]).then_inc(s_tab, 16)
                    load(ph, 0, ph == 0)
                    with sp.Fori(1, IT) as i:
                        load(ph, i)
                else:
                    if ph == 4:
                        sp.wait_ge(s_tabready, 5)
                        sp.dma_start(rows_d[0].rearrange("(a b) f -> b a f", b=P), X[:]).then_inc(s_ytab, 16)
                        sp.wait_ge(s_ygat, 16 * NB)
                        sp.dma_start(rows_d[1].rearrange("(a b) f -> b a f", b=P), Rr[:]).then_inc(s_tab, 16)
                    else:
                        sp.wait_ge(s_tabready, 6)
                        sp.dma_start(rows_d[2].rearrange("(a b) f -> b a f", b=P), Rr[:]).then_inc(s_tab, 16)
            sp.wait_ge(s_tabready, 7)
            sp.dma_start(out[0:(NB - 1) * P, :].rearrange("(a b) f -> b a f", b=P), blocks(X[:], NB - 1))\
              .then_inc(s_out, 16)
            sp.dma_start(out[(NB - 1) * P:N, :], X[0:LAST, (NB - 1) * F:NB * F]).then_inc(s_out, 16)
            sp.wait_ge(s_out, 32)

        @block.gpsimd
        def _(pool):
            def stage_next(ph, m, u, index):
                pool.tensor_tensor(stage[:, GT * u:GT * u + GT], index[:, bass.ds(m * GT, GT)], zero4[:], ALU.add)\
                    .then_inc(s_stage, 1)

            def gather(ph, i, index, table, wide, first=False):
                for u in range(UN):
                    m, v = UN * i + u, (u + 1) % UN
                    n = NG * ph + m
                    if not first:
                        if ph < 4:
                            pool.wait_ge(s_xt, n - UN + 1)
                        else:
                            pool.wait_ge(s_msk, GT * (n - UN + 1))
                    if not (first and u < UN - 1):
                        pool.wait_ge(s_g[v], 16 * GT * (IT * ph + i + (v == 0)))
                    pool.wait_ge(s_stage, (NG + 1) * ph + m + 1)
                    stage_next(ph, m + 1, v, index)
                    for q in range(GT):
                        o = gp[:, u, q, 0:PIECES * F] if wide else gf[:, u, q, :]
                        k = GT * u + q
                        pool.indirect_dma_start(o, None, table, bass.IndirectOffsetOnAxis(stage[:, k:k + 1], 0))\
                            .then_inc(s_g[u], 16)

            pool.memset(gp[:], 0.0).then_inc(s_pz, 1)
            pool.memset(zero4[:], 0).then_inc(s_pz, 1)
            pool.memset(src_i[:, NT:], 0).then_inc(s_pz, 1)
            pool.memset(dst_i[:, NT:], 0).then_inc(s_pz, 1)
            pool.wait_ge(s_pz, 4)
            pool.wait_ge(s_idx, 32)
            for ph in range(6):
                if ph == 4:
                    pool.wait_ge(s_ytab, 16)
                    for a in range(NB):
                        pool.indirect_dma_start(Rr[:, a * F:a * F + F], None, rows_d[0],
                                                bass.IndirectOffsetOnAxis(dst_i[:, a:a + 1], 0))\
                            .then_inc(s_ygat, 16)
                pool.wait_ge(s_tab, 16 * (ph + 1))
                index = dst_i if ph == 4 else src_i
                table = parts_d[ph] if ph < 4 else rows_d[ph - 3]
                if ph:
                    pool.wait_ge(s_stage, (NG + 1) * ph)
                stage_next(ph, 0, 0, index)
                gather(ph, 0, index, table, ph < 4, ph == 0)
                with pool.Fori(1, IT) as i:
                    gather(ph, i, index, table, ph < 4)

        @block.scalar
        def _(act):
            act.wait_ge(s_cst, 16)
            nc.scalar.activation(identb[:], ident, ACT.Copy).then_inc(s_const, 1)
            nc.scalar.activation(rep[:], repf, ACT.Copy).then_inc(s_const, 1)
            for c in range(CH):
                act.wait_ge(s_ein[c % 2], 16 * (c // 2 + 1))
                if c >= 2:
                    act.wait_ge(s_est[c % 2], 16 * len(STACK) * (c // 2))
                nc.scalar.activation(ea_hi[:, c % 2, :], ea_in[:, c % 2, :], ACT.Copy).then_inc(s_hi, 1)
                act.wait_ge(s_rest, c + 1)
                nc.scalar.activation(ea_mid[:, c % 2, :], ea_rest[:, c % 2, :], ACT.Copy).then_inc(s_mid, 1)

            def step(ph, i, u, first=False):
                n = NG * ph + UN * i + u
                early = first and u < 2
                act.wait_ge(s_xt, n + 1)
                if not early:
                    act.wait_ge(s_xrep, 2 * (n - 1))
                nc.scalar.activation(xts[:, u % 2, :], xT[0:PIECES * F, :], ACT.Copy).then_inc(s_xts, 1)
                for h in range(2):
                    act.wait_ge(s_lin, 2 * n + h + 1)
                    if not early:
                        act.wait_ge(s_prod, 2 * (n - 1))
                    b = bc[:, 2 * ph + h:2 * ph + h + 1]
                    nc.scalar.activation(relu[:, u % 2, h, :], lin(ph, h)[:], ACT.Relu, bias=b).then_inc(s_relu, 1)

            def copy_replicated(i, u):
                n = NG * 3 + UN * i + u
                for h in range(2):
                    act.wait_ge(s_xrep, 2 * n + h + 1)
                    nc.scalar.activation(xrs[:, u % 2, h, :], XR[h][:], ACT.Copy).then_inc(s_xrs, 1)

            def sqrt(k, r, v):
                act.wait_ge(s_var, k)
                nc.scalar.activation(r, v, ACT.Sqrt).then_inc(s_std, 1)

            for ph in range(4):
                for u in range(UN):
                    step(ph, 0, u, ph == 0)
                    if ph == 3 and u:
                        copy_replicated(0, u - 1)
                with act.Fori(1, IT) as i:
                    for u in range(UN):
                        step(ph, i, u)
                        if ph == 3:
                            copy_replicated(i if u else i - 1, (u - 1) % UN)
                if ph == 3:
                    copy_replicated(IT - 1, UN - 1)
                act.wait_ge(s_ntr, ph + 1)
                whole = ACC // P * P
                nc.scalar.activation(xnt[:, 0:whole], TR[:, 0:whole], ACT.Copy)
                nc.scalar.activation(xnt[0:ACC - whole, whole:], TR[0:ACC - whole, whole:], ACT.Copy).then_inc(s_ntc, 1)
                if ph == 2:
                    sqrt(1, st3[:], st2[:])
                if ph == 3:
                    sqrt(2, col3[:], col2[:])
                    sqrt(3, st3[:], st2[:])
            sqrt(4, st3[:], st2[:])
            sqrt(5, rdeg[:], cnt[:])
            sqrt(6, st3[:], st2[:])

        @block.vector
        def _(dve):
            done = [0]

            def link(ins):
                done[0] += 1
                ins.then_inc(s_dve, 1)
                dve.wait_ge(s_dve, done[0])

            def over_rows(v, n=NB):
                return v.unsqueeze(2).to_broadcast([P, n, F])

            dve.wait_ge(s_idx, 32)
            for i32s, place, blk in ((dst_i, dst_b, dst_a), (src_i, src_b, src_a)):
                link(nc.vector.tensor_scalar(tmp_i[:], i32s[:, 0:NT], P - 1, None, ALU.bitwise_and))
                link(nc.vector.tensor_copy(place[:], tmp_i[:]))
                link(nc.vector.tensor_scalar(tmp_i[:], i32s[:, 0:NT], P.bit_length() - 1, None, ALU.logical_shift_right))
                link(nc.vector.tensor_copy(blk[:], tmp_i[:]))
            nc.vector.memset(ones[:], 1.0)
            nc.vector.memset(Rr[:], 0.0)
            dve.wait_ge(s_w, 12 * 16)
            link(nc.vector.tensor_copy(wpart[:, 0, :], wc[:]))
            link(nc.vector.tensor_tensor(wc[:], wc[:], wpart[:, 0, :], ALU.subtract))
            link(nc.vector.tensor_copy(wpart[:, 1, :], wc[:]))
            nc.vector.tensor_tensor(wpart[:, 2, :], wc[:], wpart[:, 1, :], ALU.subtract).then_inc(s_wparts, 1)
            dve.wait_ge(s_cst, 16)
            for k in range(4):
                link(nc.vector.tensor_tensor(wdiag[:, k, :, :], wrep[:, k, :].unsqueeze(1).to_broadcast([P, 8, F]),
                                             diag.unsqueeze(2).to_broadcast([P, 8, F]), ALU.mult))

            def parts():
                v, r = blocks(X[:], NBT), blocks(Rr[:], NBT)
                link(nc.vector.tensor_copy(T48[:, :, 0:F], v))
                link(nc.vector.tensor_tensor(r, v, T48[:, :, 0:F], ALU.subtract))
                link(nc.vector.tensor_copy(T48[:, :, F:2 * F], r))
                nc.vector.tensor_tensor(T48[:, :, 2 * F:], r, T48[:, :, F:2 * F], ALU.subtract)\
                    .then_inc(s_tabready, 1)

            dve.wait_ge(s_x, 32)
            parts()
            for c in range(CH):
                dve.wait_ge(s_hi, c + 1)
                if c >= 2:
                    dve.wait_ge(s_est[c % 2], 16 * len(STACK) * (c // 2))
                nc.vector.tensor_tensor(ea_rest[:, c % 2, :], ea_in[:, c % 2, :], ea_hi[:, c % 2, :],
                                        ALU.subtract).then_inc(s_rest, 1)
                dve.wait_ge(s_mid, c + 1)
                nc.vector.tensor_tensor(ea_lo[:, c % 2, :], ea_rest[:, c % 2, :], ea_mid[:, c % 2, :],
                                        ALU.subtract).then_inc(s_lo, 1)

            def product(ph, i, u, first=False):
                n = NG * ph + UN * i + u
                m = UN * i + u
                for h in range(2):
                    if ph < 3:
                        dve.wait_ge(s_relu, 2 * n + h + 1)
                        dve.wait_ge(s_xrep, 2 * n + h + 1)
                    else:
                        dve.wait_ge(s_w2, 2 * m + h + 1)
                        dve.wait_ge(s_xrs, 2 * m + h + 1)
                    if h == 0 and not (first and u < 2):
                        dve.wait_ge(s_msg, n - 1)
                    if ph < 3:
                        nc.vector.tensor_tensor(prod[:, u % 2, h, :], relu[:, u % 2, h, :], XR[h][:], ALU.mult)\
                            .then_inc(s_prod, 1)
                    else:
                        nc.vector.scalar_tensor_tensor(prod[:, u % 2, h, :], V[h][:], bc[:, 8 + h:9 + h],
                                                       xrs[:, u % 2, h, :], ALU.add, ALU.mult).then_inc(s_prod, 1)

            def spread(ph, i, u, first=False):
                n = NG * ph + UN * i + u
                place, blk = (src_b, src_a) if ph == 4 else (dst_b, dst_a)
                r = u % 2
                if not (first and 0 <= u < 2):
                    dve.wait_ge(s_scat, n - 1)
                for q in range(GT):
                    at = bass.ds((UN * i + u) * GT + q, 1)
                    nc.vector.tensor_scalar(ohb[:, r, q, :], iota, place[:, at], None, ALU.is_equal)
                if ph < 4:
                    dve.wait_ge(s_msg, n + 1)
                else:
                    dve.wait_ge(s_g[u], 16 * GT * (IT * ph + i + 1))
                for q in range(GT):
                    at = bass.ds((UN * i + u) * GT + q, 1)
                    if ph in (0, 4):
                        nc.vector.tensor_scalar(msk[:, r, q, ACC:], iota[:, 0:NB], blk[:, at], None, ALU.is_equal)
                    m = msg(ph, r)[:, F * q:F * q + F] if ph < 4 else gf[:, u, q, :]
                    nc.vector.scalar_tensor_tensor(msk[:, r, q, 0:ACC].rearrange("p (a f) -> p a f", f=F),
                                                   over_rows(iota[:, 0:NB]), blk[:, at],
                                                   m.unsqueeze(1).to_broadcast([P, NB, F]),
                                                   ALU.is_equal, ALU.mult).then_inc(s_msk, 1)

            def edge_step(ph, i, u, phase_start=False, first=False):
                if ph < 4:
                    product(ph, i, u, first)
                    if not (phase_start and u == 0):
                        if u:
                            spread(ph, i, u - 1, first)
                        else:
                            spread(ph, i - 1, UN - 1)
                else:
                    spread(ph, i, u)

            def norm(v):
                v3, x3, y3 = blocks(v, NB), blocks(X[:], NB), blocks(Z[:], NB)
                link(nc.vector.tensor_reduce(st1[:], v3, AX, ALU.add))
                link(nc.vector.tensor_scalar(st1[:], st1[:], 1.0 / F, None, ALU.mult))
                link(nc.vector.tensor_tensor(x3, v3, over_rows(st1[:]), ALU.subtract))
                link(nc.vector.tensor_tensor(y3, x3, x3, ALU.mult))
                link(nc.vector.tensor_reduce(st2[:], y3, AX, ALU.add))
                nvar[0] += 1
                nc.vector.tensor_scalar(st2[:], st2[:], 1.0 / F, EPS, ALU.mult, ALU.add).then_inc(s_var, 1)
                dve_wait_std()
                link(nc.vector.reciprocal(st3[:], st3[:]))
                link(nc.vector.tensor_tensor(x3, x3, over_rows(st3[:]), ALU.mult))

            nvar = [0]

            def dve_wait_std():
                dve.wait_ge(s_std, nvar[0])

            def column_mean(k, v):
                link(nc.vector.tensor_reduce(col[:], v[:, 0:(NB - 1) * F].rearrange("p (a f) -> p f a", f=F), AX, ALU.add))
                nc.vector.tensor_copy(col2[:], col[:]).then_inc(s_bnin, 1)
                dve.wait_ge(s_bnout, k)
                link(nc.vector.tensor_scalar(col[:], MS[0][:, 0:F], 1.0 / N, None, ALU.mult))

            def all_rows(c):
                return c.unsqueeze(1).to_broadcast([P, NB, F])

            for ph in range(6):
                for u in range(UN):
                    edge_step(ph, 0, u, True, ph == 0)
                with dve.Fori(1, IT) as i:
                    for u in range(UN):
                        edge_step(ph, i, u)
                if ph < 4:
                    spread(ph, IT - 1, UN - 1)
                dve.wait_ge(s_scat, NG * (ph + 1))
                y3, z3, a3 = blocks(Y[:], NB), blocks(Z[:], NB), blocks(acc[:, 0:ACC], NB)
                if ph == 0:
                    link(nc.vector.tensor_scalar(cnt[:, 1, :], acc[:, ACC:ACC + NB], 1.0, None, ALU.max))
                    link(nc.vector.reciprocal(icnt[:], cnt[:, 1, :]))
                if ph == 4:
                    link(nc.vector.tensor_scalar(cnt[:, 0, :], acc[:, ACC:ACC + NB], 1.0, None, ALU.max))
                if ph < 3:
                    link(nc.vector.tensor_tensor(y3, a3, over_rows(icnt[:]), ALU.mult))
                elif ph < 5:
                    link(nc.vector.tensor_copy(Y[:], acc[:, 0:ACC]))
                if ph < 4:
                    dve.wait_ge(s_root, ph + 1)
                    link(nc.vector.tensor_tensor(Y[:], Y[:], XR[0][:, 0:ACC], ALU.add))
                if ph < 2:
                    link(nc.vector.tensor_tensor(blocks(X[:], NB), y3, all_rows(row[:, ph, :]), ALU.add))
                    parts()
                elif ph == 2:
                    link(nc.vector.tensor_tensor(y3, y3, all_rows(row[:, ph, :]), ALU.add))
                    link(nc.vector.tensor_tensor(Y[:], Y[:], X0[:, 0:ACC], ALU.add))
                    norm(Y[:])
                    parts()
                elif ph == 3:
                    link(nc.vector.tensor_tensor(y3, y3, all_rows(row[:, 3, :]), ALU.add))
                    column_mean(1, Y)
                    link(nc.vector.tensor_tensor(y3, y3, all_rows(col[:]), ALU.subtract))
                    link(nc.vector.tensor_tensor(Z[:], Y[:], Y[:], ALU.mult))
                    column_mean(2, Z)
                    nvar[0] += 1
                    nc.vector.tensor_scalar(col2[:], col[:], EPS, None, ALU.add).then_inc(s_var, 1)
                    dve_wait_std()
                    link(nc.vector.reciprocal(col3[:], col3[:]))
                    link(nc.vector.tensor_tensor(col3[:], col3[:], row[:, 4, :], ALU.mult))
                    link(nc.vector.tensor_tensor(y3, y3, all_rows(col3[:]), ALU.mult))
                    link(nc.vector.tensor_tensor(y3, y3, all_rows(row[:, 5, :]), ALU.add))
                    link(nc.vector.scalar_tensor_tensor(Y[:], Y[:], 0.0, X[:, 0:ACC], ALU.max, ALU.add))
                    norm(Y[:])
                    nc.vector.tensor_copy(st1[:], st2[:]).then_inc(s_tabready, 1)
                elif ph == 4:
                    link(nc.vector.tensor_tensor(Y[:], Y[:], X[:, 0:ACC], ALU.add))
                    norm(Y[:])
                    nvar[0] += 1
                    nc.vector.tensor_copy(st1[:], st2[:]).then_inc(s_var, 1)
                    dve_wait_std()
                    link(nc.vector.reciprocal(rdeg[:], rdeg[:]))
                    nc.vector.tensor_tensor(blocks(Rr[:], NB), blocks(X[:], NB), over_rows(rdeg[:, 0, :]), ALU.mult)\
                        .then_inc(s_tabready, 1)
                else:
                    link(nc.vector.tensor_tensor(y3, a3, over_rows(rdeg[:, 1, :]), ALU.mult))
                    link(nc.vector.tensor_tensor(Y[:], Y[:], X[:, 0:ACC], ALU.add))
                    norm(Y[:])
                    nc.vector.tensor_copy(st1[:], st2[:]).then_inc(s_tabready, 1)

        @block.tensor
        def _(pe):
            def rows_in(ph, i, u, phase_start, first):
                n = NG * ph + UN * i + u
                pe.wait_ge(s_g[u], 16 * GT * (IT * ph + i + 1))
                if not (first and u == 0):
                    pe.wait_ge(s_xts, n)
                for q in range(GT):
                    last = nc.tensor.transpose(xT[:, P * q:P * q + P], gp[:, u, q, :], identb[:])
                last.then_inc(s_xt, 1)
                if ph < 3:
                    for h in range(2):
                        first_map(ph, i, u, h, first)

            def first_map(ph, i, u, h, first):
                n = NG * ph + UN * i + u
                if h == 0:
                    pe.wait_ge(s_ea[u], 16 * (IT * ph + i + 1))
                if ph == 3:
                    pe.wait_ge(s_relu, 2 * n + h)
                elif not (first and u == 0):
                    pe.wait_ge(s_relu, 2 * (n - 1) + h + 1)
                w = wstack[:, HID * ph + P * h:HID * ph + P * h + P]
                nc.tensor.matmul(lin(ph, h)[:], w, ea_s[:, u, :], start=True, stop=True).then_inc(s_lin, 1)

            def second(ph, i, u, phase_start, h):
                n = NG * ph + UN * i + u
                if h == 0:
                    pe.wait_ge(s_relu, 2 * n + 2)
                if not (phase_start and u == 0):
                    pe.wait_ge(s_prod, 2 * (n - 1) + h + 1)
                for k in range(2):
                    last = nc.tensor.matmul(V[h][:], w2s[:, k, P * h:P * h + P], relu[:, u % 2, k, :],
                                            start=(k == 0), stop=(k == 1))
                last.then_inc(s_w2, 1)

            def replicate(ph, i, u, phase_start, first):
                n, m = NG * ph + UN * i + u, UN * i + u
                pe.wait_ge(s_xts, n + 1)
                for h in range(2):
                    if ph < 3 and not (first and u == 0):
                        pe.wait_ge(s_prod, 2 * (n - 1) + h + 1)
                    if ph == 3 and not (phase_start and u == 0):
                        pe.wait_ge(s_xrs, 2 * (m - 1) + h + 1)
                    nc.tensor.matmul(XR[h][:], rep[:, P * h:P * h + P], xts[:, u % 2, :], start=True, stop=True)\
                        .then_inc(s_xrep, 1)

            def sum_in(ph, i, u, first):
                n = NG * ph + UN * i + u
                pe.wait_ge(s_prod, 2 * n + 2)
                if ph == 3:
                    pe.wait_ge(s_msk, GT * n)
                elif not (first and 0 <= u < 2):
                    pe.wait_ge(s_msk, GT * (n - 1))
                for q in range(GT):
                    for h in range(2):
                        last = nc.tensor.matmul(msg(ph, u % 2)[:, F * q:F * q + F], prod[:, u % 2, h, P * q:P * q + P],
                                                sel, start=(h == 0), stop=(h == 1))
                last.then_inc(s_msg, 1)

            def scatter(ph, i, u, start=False, stop=False):
                n = NG * ph + UN * i + u
                wide = ACC + NB if ph in (0, 4) else ACC
                for q in range(GT):
                    pe.wait_ge(s_msk, GT * n + q + 1)
                    last = nc.tensor.matmul(acc[:, 0:wide], ohb[:, u % 2, q, :], msk[:, u % 2, q, 0:wide],
                                            start=start and q == 0, stop=stop and q == GT - 1)
                last.then_inc(s_scat, 1)

            def at(i, u, lag):
                return (i, u - lag) if u >= lag else (i - 1, u - lag + UN)

            def step(ph, i, u, phase_start=False, first=False, tail=False):
                if not tail:
                    rows_in(ph, i, u, phase_start, first)
                if ph == 3:
                    j, v = at(i, u, 1)
                    for h in range(2):
                        if not tail:
                            first_map(ph, i, u, h, first)
                        if not (phase_start and u < 1) and not (tail and u > 0):
                            second(ph, j, v, phase_start, h)
                for lag in (1, 2, 3):
                    j, v = at(i, u, lag)
                    if (phase_start and u < lag) or (tail and lag <= u):
                        continue
                    if lag == 1:
                        replicate(ph, j, v, phase_start, first)
                    elif lag == 2:
                        sum_in(ph, j, v, first)
                    else:
                        scatter(ph, j, v, phase_start and u == lag, tail and u == lag - 1)

            pe.wait_ge(s_const, 2)
            pe.wait_ge(s_wstack, 16 * len(WSTACK))
            pe.wait_ge(s_w, 12 * 16)
            for ph in range(6):
                if ph < 4:
                    for u in range(UN):
                        step(ph, 0, u, True, ph == 0)
                    with pe.Fori(1, IT) as i:
                        for u in range(UN):
                            step(ph, i, u)
                    for u in range(3):
                        step(ph, IT, u, tail=True)
                    pe.wait_ge(s_prod, 2 * NG * (ph + 1))
                    pe.wait_ge(s_tabready, ph + 1)
                    for c in range(4):
                        k = min(P, ACC - P * c)
                        last = nc.tensor.transpose(TR[0:k, P * c:P * c + P], X[:, P * c:P * c + k], ident)
                    last.then_inc(s_ntr, 1)
                    pe.wait_ge(s_ntc, ph + 1)
                    for c in range(4):
                        k = min(P, ACC - P * c)
                        r = wdiag[:, ph, :, :].rearrange("p a f -> p (a f)")[0:k, 0:k]
                        last = nc.tensor.matmul(XR[0][:, P * c:P * c + k], xnt[0:k, P * c:P * c + P], r,
                                                start=True, stop=True)
                    last.then_inc(s_root, 1)
                else:
                    for u in range(UN):
                        scatter(ph, 0, u, start=u == 0)
                    with pe.Fori(1, IT - 1) as i:
                        for u in range(UN):
                            scatter(ph, i, u)
                    for u in range(UN):
                        scatter(ph, IT - 1, u, stop=u == UN - 1)
                if ph == 3:
                    for k, v in enumerate((Y, Z)):
                        pe.wait_ge(s_bnin, k + 1)
                        nc.tensor.matmul(MS[0][:, 0:F], ones[:], col2[:], start=True, stop=False)
                        nc.tensor.matmul(MS[0][:, 0:F], live, v[:, (NB - 1) * F:ACC], start=False, stop=True)\
                            .then_inc(s_bnout, 1)


def kernel(**a):
    import numpy as np
    import concourse.bacc as bacc
    from concourse import mybir as mb
    from concourse.bass_utils import run_bass_kernel_spmd as run

    def padded(v, n, fill):
        return np.pad(v, [(0, n - v.shape[0])] + [(0, 0)] * (v.ndim - 1), constant_values=fill)

    names = [f"L0_gnn_Wn{k}" for k in (1, 2, 3)] + ["L1_gnn_W1"]
    biases = [f"L0_gnn_bn{k}" for k in (1, 2, 3)] + ["L1_gnn_b1", "L1_gnn_b2"]
    roots = [f"L0_gnn_Wr{k}" for k in (1, 2, 3)] + ["L1_gnn_root"]
    lines = [f"L0_gnn_b{k}" for k in (1, 2, 3)] + ["L1_gnn_bias", "L1_gnn_gamma", "L1_gnn_beta"]
    place = np.arange(P)
    consts = np.zeros((P, 5 * P + F + 8), np.float32)
    consts[:, 0:P] = np.eye(P)
    consts[:, P:2 * P] = place
    consts[:LAST, 2 * P:3 * P] = 1
    consts[:, 3 * P:3 * P + F] = place[:, None] % F == np.arange(F)
    i_of = np.arange(2 * P) // F
    consts[:PIECES * F, 3 * P + F:5 * P + F] = place[:PIECES * F, None] % F == i_of
    consts[:, 5 * P + F:] = place[:, None] // F == np.arange(8)
    arrays = {
        "x": padded(np.asarray(a["x"]), NPAD, 0),
        "srcT": padded(np.asarray(a["src"]), EP, NB * P).reshape(NT, P).T,
        "dstT": padded(np.asarray(a["dst"]), EP, NB * P).reshape(NT, P).T,
        "eaT": padded(np.asarray(a["edge_attr_16"]), EP, 0).T.reshape(P, EC),
        "wcat": np.concatenate([np.asarray(a[k]) for k in names], axis=1),
        "bcol": np.concatenate([np.asarray(a[k]).reshape(2, P) for k in biases], axis=0).T,
        "rows": np.concatenate([np.asarray(a[k]) for k in lines])[None, :],
        "wroot": np.stack([np.asarray(a[k]) for k in roots], axis=1),
        "w2": np.asarray(a["L1_gnn_W2"]),
        "consts": consts,
    }
    arrays = {f"in_{k}": np.ascontiguousarray(v) for k, v in arrays.items()}
    nc = bacc.Bacc("TRN2", target_bir_lowering=False, num_devices=1)
    args = [nc.dram_tensor(k, v.shape, mb.dt.from_np(v.dtype), kind="ExternalInput").ap() for k, v in arrays.items()]
    out = nc.dram_tensor("out_x", (N, F), mb.dt.float32, kind="ExternalOutput").ap()
    gnn_kernel(nc, *args, out)
    return run(nc, [arrays], core_ids=[0]).results[0]["out_x"]
```

```python
import concourse.bass as bass
from concourse import mybir
from contextlib import ExitStack

N = 3125
E = 100000
F = 16
HID = F * F
P = 128
PIECES = 3
GT = 4
GE = GT * P
UN = 4
NB = -(-N // P)
BN = N // NB
assert BN * NB == N
DSHIFT = 19
DMUL = -(-(1 << DSHIFT) // BN)
assert all(k * DMUL >> DSHIFT == k // BN for k in range(N)) and N * DMUL < 1 << 24
LANES = next(k for k in range(P, 0, -1) if E % k == 0)
PER = E // LANES
NG = -(-((E + NB * (P - 1)) // P) // (UN * GT)) * UN
NT = NG * GT
IT = NG // UN
ACC = NB * F
NBX = 32
SLOT = 64
FAST = 3
STACK = (0, 0, 0, 1, 1, 2)
WSTACK = (0, 1, 2, 0, 1, 0)
KO = len(STACK) * F
KS = KO + PIECES
REC = KO + 8
LAG = UN + 2
PAD = GT * LAG
CK = 20
NC = PER // CK
EMPTY_DST = NB * P
EMPTY_PLACE = 200
EPS = 1e-5
NCH = -(-NT // P)
CW = 4 * P + NB + 8


def gnn_kernel(nc, x, src, dst, dst_n, ea, wcat, bias3, rows, wroot, w2, consts, iota_h, out):
    fp32, bf16, i32, i16 = mybir.dt.float32, mybir.dt.bfloat16, mybir.dt.int32, mybir.dt.int16
    ALU, ACT, AX = mybir.AluOpType, mybir.ActivationFunctionType, mybir.AxisListType.X
    TILES = list(range(GT))

    ctx = ExitStack()
    with ctx:
        def sb(name, shape, dt):
            return ctx.enter_context(nc.sbuf_tensor(name, shape, dt))

        def pb(name, banks=1):
            return ctx.enter_context(nc.psum_tensor(name, [P, 512 * banks], fp32))

        def sem(name):
            return ctx.enter_context(nc.semaphore(name))

        rec_d = nc.dram_tensor("rec_d", [NG * GE, REC], bf16).ap()
        place_d = nc.dram_tensor("place_d", [NT, P], bf16).ap()
        rel_d = nc.dram_tensor("rel_d", [NT, P], i16).ap()
        low_d = nc.dram_tensor("low_d", [NCH, P], fp32).ap()
        span_d = nc.dram_tensor("span_d", [1, P], fp32).ap()
        rows_d = nc.dram_tensor("rows_d", [N, F], fp32).ap()

        cst = sb("cst", [P, CW], fp32)
        ident = cst[:, 0:P]
        live = cst[:, P:2 * P]
        before = cst[:, 2 * P:3 * P]
        iota = cst[:, 3 * P:4 * P]
        column = cst[:, 4 * P:4 * P + NB]
        diag = cst[:, 4 * P + NB:4 * P + NB + 8]
        identb = sb("identb", [P, P], bf16)
        iota_i = sb("iota_i", [P, NB * P], i16)
        ones = sb("ones", [P, P], fp32)
        zeros = sb("zeros", [P, 512], bf16)
        wc = sb("wc", [F, 4 * HID], fp32)
        wpart = sb("wpart", [F, PIECES, 4 * HID], bf16)
        bw = sb("bw", [1, 4 * HID], fp32)
        bpart = sb("bpart", [1, PIECES, 4 * HID], bf16)
        b2r = sb("b2r", [P, HID], fp32)
        wstack = sb("wstack", [KS, 4 * HID], bf16)
        row = sb("row", [P, 6, F], fp32)
        wrep = sb("wrep", [P, 4, F], fp32)
        wdiag = sb("wdiag", [P, 4, 8, F], fp32)
        w2s = sb("w2s", [P, 2, HID], fp32)

        ints = sb("ints", [P, 4 * PER], i32)
        src_i, dst_i, tmp_i, tmp2_i = (ints[0:LANES, PER * k:PER * (k + 1)] for k in range(4))
        dstn_i = sb("dstn_i", [P, NB], i32)
        blk = sb("blk", [LANES, PER], fp32)
        pair = sb("pair", [LANES, PER, 2], fp32)
        work = sb("work", [P, NB * PER], bf16)
        same = work[0:LANES, 0:NB * PER].rearrange("l (a k) -> l a k", a=NB)
        count = sb("count", [LANES, PER], fp32)
        pos = sb("pos", [LANES, PER], fp32)
        hist = sb("hist", [LANES, NB], fp32)
        grp = sb("grp", [LANES, NB], fp32)
        grp_i = sb("grp_i", [LANES, NB], i32)
        gend = sb("gend", [LANES, NB], fp32)
        base = sb("base", [LANES, NB], fp32)
        pos_i = sb("pos_i", [LANES, PER + CK], i32)
        zero_i = sb("zero_i", [LANES, CK], i32)
        stage = sb("stage", [LANES, 2, CK], i32)
        ea_in = sb("ea_in", [LANES, 2, CK, F], fp32)
        ea_r = sb("ea_r", [LANES, 2, CK, F], fp32)
        rec = sb("rec", [LANES, 2, CK, REC], bf16)
        blank = sb("blank", [P, UN * GT, REC], bf16)

        tab = sb("tab", [P, 2, NT], fp32)
        dst2_i = sb("dst2_i", [P, NT], i32)
        dblk = sb("dblk", [P, NT], fp32)
        dblk2 = sb("dblk2", [P, NT], fp32)
        low = sb("low", [P, NCH], fp32)
        high = sb("high", [P, NCH], fp32)
        span = sb("span", [P, 1], fp32)
        spans = sb("spans", [P, P], fp32)
        far = sb("far", [P, 1], fp32)
        near = sb("near", [P, 1], fp32)
        far_i = sb("far_i", [1, 1], i32)
        lowr = sb("lowr", [P, NCH * P], fp32)
        rel = sb("rel", [P, NT], fp32)
        src2_i = sb("src2_i", [P, NT], i32)
        starts = sb("starts", [1, 2 * PAD + NT], i32)
        sources = sb("sources", [1, 2 * PAD + NT], i32)
        turned_b = sb("turned_b", [P, NCH, P], bf16)
        turned_i = sb("turned_i", [P, NCH, P], i16)

        er = sb("er", [P, UN, GT, REC], bf16)
        prow = sb("prow", [P, UN, GE], bf16)
        rrow = sb("rrow", [P, UN, GE], i16)
        eT = sb("eT", [REC, 2, GE], bf16)
        ohT = sb("ohT", [P, 2, FAST, GE], bf16)
        xparts = sb("xparts", [P, 2, GT, PIECES, F], fp32)
        xg = sb("xg", [P, UN, GT, F], fp32)
        hs = work[:, 0:4 * 2 * GE].bitcast(fp32).rearrange("p (r h e) -> p r h e", r=2, h=2)
        wr = work[:, 8 * GE:24 * GE].bitcast(fp32).rearrange("p (r q w) -> p r q w", r=UN, q=GT)
        msg = sb("msg", [P, UN, GT, F], fp32)
        rest = sb("rest", [P, UN, GT, F], fp32)
        m48 = sb("m48", [P, UN, GT, SLOT], bf16)
        oh = work[:, 24 * GE:24 * GE + UN * GT * FAST * P].rearrange("p (r q w) -> p r q w", r=UN, q=GT)
        ohg = ints[:].bitcast(bf16)[:, 0:2 * NB * P].rearrange("p (r w) -> p r w", r=2)

        X = sb("X", [P, NBX * F], fp32)
        X0 = sb("X0", [P, ACC], fp32)
        T48 = sb("T48", [P, NBX * PIECES * F], bf16)
        Rr = sb("Rr", [P, NBX * F], fp32)
        Pr = sb("Pr", [P, NBX * F], fp32)
        Y = sb("Y", [P, ACC], fp32)
        Z = sb("Z", [P, ACC], fp32)
        xnt = sb("xnt", [P, 512], fp32)
        cnt = sb("cnt", [P, 2, NB], fp32)
        icnt = sb("icnt", [P, NB], fp32)
        rdeg = sb("rdeg", [P, 2, NB], fp32)
        st1 = sb("st1", [P, NB], fp32)
        st2 = sb("st2", [P, NB], fp32)
        st3 = sb("st3", [P, NB], fp32)
        col = sb("col", [P, F], fp32)
        col2 = sb("col2", [P, F], fp32)
        col3 = sb("col3", [P, F], fp32)

        W = [pb("W0"), pb("W1")]
        TX = pb("TX")
        H = pb("H")
        acc = pb("acc", 4)
        acc3 = acc[:].rearrange("p (a s) -> p a s", s=SLOT)
        t_out = TX[:, 0:GE // 2].bitcast(bf16)

        def x_out(wide):
            return TX[:, GE // 2:GE // 2 + GT * wide]

        s_cst, s_x, s_idx, s_w, s_out = sem("s_cst"), sem("s_x"), sem("s_idx"), sem("s_wload"), sem("s_out")
        s_ein = [sem(f"s_ein{k}") for k in range(2)]
        s_blank, s_fill = sem("s_blank"), sem("s_fill")
        s_hist, s_pre, s_rows = sem("s_hist"), sem("s_pre"), sem("s_rows")
        s_hi, s_rest, s_mid, s_rec = sem("s_hi"), sem("s_rest"), sem("s_mid"), sem("s_rec")
        s_zero, s_stage = sem("s_zero"), sem("s_stage")
        s_sc = [sem(f"s_sc{k}") for k in range(2)]
        s_ex = [sem(f"s_ex{k}") for k in range(2)]
        s_exd = sem("s_exd")
        s_turn, s_turned, s_low, s_lowd = sem("s_turn"), sem("s_turned"), sem("s_low"), sem("s_lowd")
        s_lows, s_dir, s_dird = sem("s_lows"), sem("s_dir"), sem("s_dird")
        s_wparts, s_wstack = sem("s_wparts"), sem("s_wstack")
        s_dve, s_const, s_tabready = sem("s_dve"), sem("s_const"), sem("s_tabready")
        s_er = [sem(f"s_er{k}") for k in range(UN)]
        s_oht, s_tx, s_txc, s_lin = sem("s_oht"), sem("s_tx"), sem("s_txc"), sem("s_lin")
        s_h, s_relu = sem("s_h"), sem("s_relu")
        s_wr, s_red, s_mhi, s_r1, s_mmid, s_lo = (sem("s_wr"), sem("s_red"), sem("s_mhi"), sem("s_r1"),
                                                    sem("s_mmid"), sem("s_lo"))
        s_xpart, s_xg, s_pprod = sem("s_xpart"), sem("s_xg"), sem("s_pprod")
        s_oh, s_scat = sem("s_oh"), sem("s_scat")
        s_ohg, s_gsc = sem("s_ohg"), sem("s_gsc")
        s_yoht, s_yx = sem("s_yoht"), sem("s_yx")
        s_ntr, s_ntc, s_root = sem("s_ntr"), sem("s_ntc"), sem("s_root")
        s_bnin, s_bnout = sem("s_bnin"), sem("s_bnout")
        s_var, s_std = sem("s_var"), sem("s_std")
        s_yst, s_ygat, s_yrows = sem("s_yst"), sem("s_ygat"), sem("s_yrows")
        s_rel, s_tabs, s_ohs = sem("s_rel"), sem("s_tabs"), sem("s_ohs")
        s_closed = sem("s_closed")
        s_clear = sem("s_clear")

        block = ctx.enter_context(nc.Block())

        def blocks(ap, a):
            return ap.rearrange("p (a f) -> p a f", f=F)[:, 0:a, :]

        def behind(i, u, lag):
            j, v = i + (u - lag) // UN, (u - lag) % UN
            if isinstance(j, int) and not 0 <= j < IT:
                return None
            return j, v

        def positive(v):
            return not isinstance(v, int) or v > 0

        def turns(eng, step):
            for i in range(2):
                for u in range(UN):
                    step(i, u)
            with eng.Fori(2, IT) as i:
                for u in range(UN):
                    step(i, u)
            for u in range(LAG):
                step(IT + u // UN, u % UN)


        @block.sync
        def _(sp):
            sp.dma_start(src_i[:], src).then_inc(s_idx, 16)
            sp.dma_start(dst_i[:], dst).then_inc(s_idx, 16)
            sp.dma_start(cst[:], consts).then_inc(s_cst, 16)
            sp.dma_start(iota_i[:], iota_h.to_broadcast([P, NB * P])).then_inc(s_cst, 16)
            sp.wait_ge(s_blank, 1)
            turn_recs = rec_d.rearrange("(i p t) c -> i p (t c)", p=P, t=UN * GT)
            group_recs = rec_d.rearrange("(i p u q) c -> i u p (q c)", p=P, u=UN, q=GT)
            with sp.Fori(0, IT) as i:
                sp.dma_start(turn_recs[bass.ds(i, 1), :, :].rearrange("a p c -> (a p) c"),
                             blank[:].rearrange("p q c -> p (q c)")).then_inc(s_fill, 16)
            eav = ea.rearrange("l (c k) -> l c k", k=CK * F)

            def ea_load(c, r, wait=None):
                if wait is not None:
                    sp.wait_ge(s_rec, wait)
                sp.dma_start(ea_in[:, r, :, :].rearrange("l k f -> l (k f)").unsqueeze(1), eav[:, bass.ds(c, 1), :])\
                  .then_inc(s_ein[r], 16)

            for r in range(2):
                ea_load(r, r)
            sp.wait_ge(s_clear, 1)
            sp.dma_start(X[0:BN, 0:ACC], x.rearrange("(a b) f -> b a f", b=BN)).then_inc(s_x, 16)
            sp.dma_start(X0[0:BN, :], x.rearrange("(a b) f -> b a f", b=BN)).then_inc(s_x, 16)
            sp.dma_start(dstn_i[0:BN, :], dst_n).then_inc(s_x, 16)
            sp.dma_start(wc[:], wcat).then_inc(s_w, 16)
            sp.dma_start(bw[:], bias3[:, 0:4 * HID]).then_inc(s_w, 16)
            sp.dma_start(b2r[:], bias3[:, 4 * HID:].to_broadcast([P, HID])).then_inc(s_w, 16)
            sp.dma_start(row[:].rearrange("p k f -> p (k f)"), rows.to_broadcast([P, 6 * F])).then_inc(s_w, 16)
            sp.dma_start(w2s[:], w2.rearrange("(k p) n -> p k n", p=P)).then_inc(s_w, 16)
            for a in range(8):
                sp.dma_start(wrep[F * a:F * a + F, :, :], wroot).then_inc(s_w, 16)
            with sp.Fori(1, NC // 2) as c2:
                for r in range(2):
                    ea_load(c2 * 2 + r, r, c2 * 2 + r - 1)
            sp.wait_ge(s_wparts, 1)
            for k, q in enumerate(WSTACK):
                sp.dma_start(wstack[F * k:F * k + F, :], wpart[:, q, :]).then_inc(s_wstack, 16)
            for q in range(PIECES):
                sp.dma_start(wstack[KO + q:KO + q + 1, :], bpart[:, q, :]).then_inc(s_wstack, 16)
            for r in range(2):
                sp.wait_ge(s_sc[r], 16 * CK * (NC // 2))

            def sorted_turn(i, r):
                sp.dma_start((er[:].rearrange("p u q c -> p (u q c)"), blank[:].rearrange("p a c -> p (a c)"))[r],
                             turn_recs[bass.ds(i, 1), :, :].rearrange("a p c -> (a p) c")).then_inc(s_ex[r], 16)

            for r in range(2):
                sorted_turn(r, r)
            with sp.Fori(1, IT // 2) as i2:
                for r in range(2):
                    sp.wait_ge(s_exd, 2 * i2 + r - 1)
                    sorted_turn(2 * i2 + r, r)
            if IT % 2:
                sp.wait_ge(s_exd, IT - 2)
                sorted_turn(IT - 1, 0)

            def records(u, i, s):
                sp.dma_start(er[:, u, :, :].rearrange("p q c -> p (q c)"),
                             group_recs[bass.ds(i, 1), u, :, :].rearrange("a p c -> (a p) c")).then_inc(s, 16)

            sp.wait_ge(s_low, 1)
            sp.dma_start(low_d.rearrange("c p -> p c"), low[:], allow_slow_non_contiguous=True).then_inc(s_lowd, 16)
            sp.dma_start(span_d.rearrange("a p -> p a"), span[:], allow_slow_non_contiguous=True).then_inc(s_lowd, 16)
            sp.wait_ge(s_lowd, 32)
            sp.dma_start(lowr[:], low_d.rearrange("c p -> (c p)").unsqueeze(0).to_broadcast([P, NCH * P]))\
              .then_inc(s_lows, 16)
            sp.dma_start(spans[:], span_d.to_broadcast([P, P])).then_inc(s_lows, 16)
            for k, (turned, d) in enumerate(((turned_b, place_d), (turned_i, rel_d))):
                sp.wait_ge(s_dir, k + 1)
                whole = (NCH - 1) * P
                sp.dma_start(d[0:whole, :].rearrange("(c t) e -> t c e", t=P), turned[:, 0:NCH - 1, :])\
                  .then_inc(s_dird, 16)
                sp.dma_start(d[whole:NT, :], turned[0:NT - whole, NCH - 1, :]).then_inc(s_dird, 16)
            sp.wait_ge(s_dird, 64)
            places = place_d.rearrange("(g q) e -> g (q e)", q=GT)
            rels = rel_d.rearrange("(g q) e -> g (q e)", q=GT)

            def load(ph, i, first=False):
                for u in range(UN):
                    n = NG * ph + UN * i + u
                    g = UN * i + u
                    if not first:
                        sp.wait_ge(s_tx, n - UN + 1)
                    if ph < 4:
                        records(u, i, s_er[u])
                    if ph == 4:
                        sp.dma_start(rrow[:, u, :], rels[bass.ds(g, 1), :].to_broadcast([P, GE])).then_inc(s_er[u], 16)
                    else:
                        sp.dma_start(prow[:, u, :], places[bass.ds(g, 1), :].to_broadcast([P, GE]))\
                          .then_inc(s_er[u], 16)

            for ph in range(6):
                if ph == 4:
                    sp.wait_ge(s_yst, 1)
                    sp.dma_start(rows_d.rearrange("(a b) f -> b a f", b=BN), blocks(X[0:BN, :], NB)).then_inc(s_ygat, 16)
                load(ph, 0, ph == 0)
                with sp.Fori(1, IT) as i:
                    load(ph, i)
            sp.wait_ge(s_tabready, 7)
            sp.dma_start(out.rearrange("(a b) f -> b a f", b=BN), blocks(X[0:BN, :], NB)).then_inc(s_out, 16)
            sp.wait_ge(s_out, 16)

        def loads_done(ph, i):
            before_ph = 32 * IT * min(ph, 4) + 16 * IT * max(ph - 4, 0)
            return before_ph + (32 if ph < 4 else 16) * (i + 1)

        def product(eng, u, a, b):
            w = wr[:, u, a:b, :].rearrange("p q (i o) -> p (q i) o", o=F)
            xi = xg[:, u, a:b, :].rearrange("p q f -> p (q f)").unsqueeze(2).to_broadcast([P, (b - a) * F, F])
            return eng.tensor_tensor(w, w, xi, ALU.mult)

        BY_DST = {0: 0, 1: 1, 2: 2, 3: 3, 5: 4}

        @block.gpsimd
        def _(pool):
            pool.memset(blank[:], 0.0).then_inc(s_zero, 1)
            pool.memset(rec[:], 1.0).then_inc(s_zero, 1)
            pool.memset(zero_i[:], 0).then_inc(s_zero, 1)
            pool.memset(m48[:], 1.0).then_inc(s_zero, 1)
            pool.wait_ge(s_zero, 4)
            blank_f = blank[:].rearrange("p q c -> p (q c)").bitcast(fp32).rearrange("p (q c) -> p q c", q=UN * GT)
            pool.memset(blank_f[:, :, KO // 2 + 2:KO // 2 + 3], float(EMPTY_DST)).then_inc(s_zero, 1)
            pool.wait_ge(s_zero, 5)
            pool.memset(blank_f[:, :, KO // 2 + 3:KO // 2 + 4], float(EMPTY_PLACE)).then_inc(s_blank, 1)
            pool.wait_ge(s_rows, 1)

            HK = CK // 2

            def stage_half(c, r, h):
                pool.tensor_tensor(stage[:, r, HK * h:HK * h + HK], pos_i[:, bass.ds(c * CK + HK * h, HK)],
                                   zero_i[:, 0:HK], ALU.add).then_inc(s_stage, 1)

            def scatter_half(r, h):
                for k in range(HK * h, HK * h + HK):
                    pool.indirect_dma_start(rec_d, bass.IndirectOffsetOnAxis(stage[:, r, k:k + 1], 0),
                                            rec[:, r, k, :], None).then_inc(s_sc[r], 16)

            def scatter_chunks(c2, first=False):
                for r in range(2):
                    c = c2 * 2 + r
                    pool.wait_ge(s_rec, c + 1)
                    pool.wait_ge(s_stage, 2 * c + 1)
                    stage_half(c, r, 1)
                    scatter_half(r, 0)
                    if not (first and r == 0):
                        pool.wait_ge(s_sc[1 - r], 16 * CK * (c2 + r))
                    pool.wait_ge(s_stage, 2 * c + 2)
                    stage_half(c + 1, 1 - r, 0)
                    scatter_half(r, 1)

            pool.wait_ge(s_fill, 16 * IT)
            stage_half(0, 0, 0)
            scatter_chunks(0, True)
            with pool.Fori(1, NC // 2) as c2:
                scatter_chunks(c2)

            def step(ph, i, u):
                if behind(i, u, 0):
                    n = NG * ph + UN * i + u
                    pool.wait_ge(s_txc, n + 1)
                    if positive(n - UN + 1):
                        pool.wait_ge(s_pprod, n - UN + 1)
                    xp = xparts[:, u % 2, :, :, :]
                    pool.tensor_tensor(xg[:, u, :, :], xp[:, :, 0, :], xp[:, :, 1, :], ALU.add)\
                        .then_inc(s_xpart, 1)
                    pool.wait_ge(s_xpart, n + 1)
                    pool.tensor_tensor(xg[:, u, :, :], xg[:, u, :, :], xp[:, :, 2, :], ALU.add)\
                        .then_inc(s_xg, 1)
                if behind(i, u, 1):
                    j, v = behind(i, u, 1)
                    n = NG * ph + UN * j + v
                    pool.wait_ge(s_xg, n + 1)
                    for a, b in ((0, 2), (2, GT)):
                        pool.wait_ge(s_wr, 2 * n + a // 2 + 1)
                        last = product(pool, v, a, b)
                    last.then_inc(s_pprod, 1)

            for ph in range(4):
                turns(pool, lambda i, u: step(ph, i, u))
            pool.wait_ge(s_ygat, 16)
            for a in range(NB):
                pool.indirect_dma_start(Rr[0:BN, a * F:a * F + F], None, rows_d,
                                        bass.IndirectOffsetOnAxis(dstn_i[0:BN, a:a + 1], 0)).then_inc(s_yrows, 16)

        @block.scalar
        def _(act):
            act.wait_ge(s_cst, 32)
            nc.scalar.activation(identb[:], ident, ACT.Copy).then_inc(s_const, 1)

            def form_chunk(c, r, turn, first=False):
                act.wait_ge(s_ein[r], 16 * (turn + 1))
                if not first:
                    act.wait_ge(s_sc[r], 16 * CK * turn)
                high = ea_in[:, r, :, :].unsqueeze(2).to_broadcast([LANES, CK, 3, F])
                nc.scalar.activation(rec[:, r, :, 0:3 * F].rearrange("l k (j f) -> l k j f", f=F), high, ACT.Copy)\
                    .then_inc(s_hi, 1)
                act.wait_ge(s_rest, c + 1)
                middle = ea_r[:, r, :, :].unsqueeze(2).to_broadcast([LANES, CK, 2, F])
                nc.scalar.activation(rec[:, r, :, 3 * F:5 * F].rearrange("l k (j f) -> l k j f", f=F), middle,
                                     ACT.Copy).then_inc(s_mid, 1)

            act.wait_ge(s_zero, 2)
            for r in range(2):
                form_chunk(r, r, 0, True)
            with act.Fori(1, NC // 2) as c2:
                for r in range(2):
                    form_chunk(c2 * 2 + r, r, c2)

            def matrices(ph, i, u, b):
                n = NG * ph + UN * i + u
                act.wait_ge(s_lin, 2 * n + b + 1)
                if positive(n - UN + 1):
                    act.wait_ge(s_red, n - UN + 1)
                nc.scalar.activation(wr[:, u, 2 * b:2 * b + 2, :].rearrange("p q w -> p (q w)"), W[b][:],
                                     ACT.Relu).then_inc(s_wr, 1)

            def step(ph, i, u):
                if behind(i, u, 4):
                    j, v = behind(i, u, 4)
                    n = NG * ph + UN * j + v
                    act.wait_ge(s_red, n + 1)
                    if positive(n - UN + 1):
                        act.wait_ge(s_scat, n - UN + 1)
                    nc.scalar.activation(m48[:, v, :, 0:F], msg[:, v, :, :], ACT.Copy).then_inc(s_mhi, 1)
                if behind(i, u, 5):
                    j, v = behind(i, u, 5)
                    n = NG * ph + UN * j + v
                    act.wait_ge(s_r1, n + 1)
                    nc.scalar.activation(m48[:, v, :, F:2 * F], rest[:, v, :, :], ACT.Copy).then_inc(s_mmid, 1)
                if behind(i, u, 0):
                    n = NG * ph + UN * i + u
                    act.wait_ge(s_tx, n + 1)
                    if positive(n - 1):
                        act.wait_ge(s_lin, 2 * (n - 1))
                        act.wait_ge(s_xg, n - 1)
                    nc.scalar.activation(eT[:, u % 2, :], t_out[0:REC, :], ACT.Copy)
                    nc.scalar.activation(xparts[:, u % 2, :, :, :].rearrange("p q c f -> p (q c f)"),
                                         x_out(PIECES * F), ACT.Copy).then_inc(s_txc, 1)
                if ph == 3 and behind(i, u, 0):
                    for h in range(2):
                        act.wait_ge(s_h, 2 * (UN * i + u) + h + 1)
                        nc.scalar.activation(hs[:, u % 2, h, :], H[:], ACT.Relu).then_inc(s_relu, 1)
                if ph < 3 and behind(i, u, 1):
                    for b in range(2):
                        matrices(ph, *behind(i, u, 1), b)

            def sqrt(k, r, v):
                act.wait_ge(s_var, k)
                nc.scalar.activation(r, v, ACT.Sqrt).then_inc(s_std, 1)

            act.wait_ge(s_zero, 4)
            for ph in range(4):
                turns(act, lambda i, u: step(ph, i, u))
                act.wait_ge(s_ntr, ph + 1)
                whole = ACC // P * P
                nc.scalar.activation(xnt[:, 0:whole], W[0][:, 0:whole], ACT.Copy)
                nc.scalar.activation(xnt[0:ACC - whole, whole:], W[0][0:ACC - whole, whole:], ACT.Copy)\
                    .then_inc(s_ntc, 1)
                if ph == 2:
                    sqrt(1, st3[:], st2[:])
                if ph == 3:
                    sqrt(2, col3[:], col2[:])
                    sqrt(3, st3[:], st2[:])

            def rows_step(ph, i):
                for u in range(UN):
                    n = NG * ph + UN * i + u
                    act.wait_ge(s_tx, n + 1)
                    act.wait_ge(s_scat, n - UN + 1)
                    nc.scalar.activation(m48[:, u, :, 0:PIECES * F],
                                         x_out(PIECES * F).rearrange("p (q c) -> p q c", q=GT), ACT.Copy)\
                        .then_inc(s_txc, 1)

            for ph in (4, 5):
                rows_step(ph, 0)
                with act.Fori(1, IT) as i:
                    rows_step(ph, i)
                if ph == 4:
                    sqrt(4, st3[:], st2[:])
                    sqrt(5, rdeg[:], cnt[:])
            sqrt(6, st3[:], st2[:])

        @block.vector
        def _(dve):
            done = [0]
            nvar = [0]

            def link(ins):
                done[0] += 1
                ins.then_inc(s_dve, 1)
                dve.wait_ge(s_dve, done[0])

            def over_rows(v, n=NB):
                return v.unsqueeze(2).to_broadcast([P, n, F])

            def all_rows(c):
                return c.unsqueeze(1).to_broadcast([P, NB, F])

            V = nc.vector
            V.memset(ones[:], 1.0)
            V.memset(starts[:], 0)
            V.memset(sources[:], 0)
            V.memset(zeros[:], 0.0)
            V.memset(X[:], 0.0)
            V.memset(X0[:], 0.0).then_inc(s_clear, 1)
            V.memset(Rr[:], 0.0)
            V.memset(low[:], 0.0)
            V.memset(high[:], 0.0)
            V.memset(pos_i[:, PER:], 0)
            link(V.memset(pos[:], 0.0))
            dve.wait_ge(s_idx, 32)
            shift = P.bit_length() - 1
            for v in (dst_i, src_i):
                link(V.tensor_scalar(tmp_i[:], v[:], DMUL, None, ALU.mult))
                link(V.tensor_scalar(tmp_i[:], tmp_i[:], DSHIFT, None, ALU.logical_shift_right))
                if v is dst_i:
                    link(V.scalar_tensor_tensor(pair[:, :, 0], tmp_i[:], float(P - BN), v[:], ALU.mult, ALU.add))
            link(V.tensor_copy(blk[:], tmp_i[:]))
            link(V.scalar_tensor_tensor(pair[:, :, 1], tmp_i[:], float(2 * P - BN), src_i[:], ALU.mult, ALU.add))
            for a in range(NB):
                link(V.tensor_scalar(same[:, a, :], blk[:], float(a), None, ALU.is_equal))
                link(V.tensor_tensor_scan(count[:], same[:, a, :], same[:, a, :], 0.0, ALU.add, ALU.max))
                V.tensor_copy(hist[:, a:a + 1], count[:, PER - 1:PER])
                link(V.copy_predicated(pos[:], same[:, a, :].bitcast(i16), count[:]))
            V.tensor_copy(grp[:], hist[:]).then_inc(s_hist, 1)
            dve.wait_ge(s_cst, 32)
            dve.wait_ge(s_pre, 1)
            link(V.tensor_scalar(grp[:], W[1][0:LANES, 0:NB], float(P - 1), None, ALU.add))
            link(V.tensor_copy(grp_i[:], grp[:]))
            link(V.tensor_scalar(grp_i[:], grp_i[:], shift, None, ALU.logical_shift_right))
            link(V.tensor_copy(grp[:], grp_i[:]))
            link(V.tensor_tensor_scan(gend[:], grp[:], grp[:], 0.0, ALU.add, ALU.max))
            link(V.tensor_tensor(base[:], gend[:], grp[:], ALU.subtract))
            link(V.tensor_scalar(base[:], base[:], float(P), -1.0, ALU.mult, ALU.add))
            link(V.tensor_tensor(base[:], base[:], W[0][0:LANES, 0:NB], ALU.add))
            for a in range(NB):
                link(V.scalar_tensor_tensor(pos[:], same[:, a, :], base[:, a:a + 1], pos[:], ALU.mult, ALU.add))
            at_i = pos_i[:, 0:PER]
            turn_edges = UN * GT * P
            link(V.tensor_copy(at_i, pos[:]))
            link(V.tensor_scalar(tmp_i[:], at_i, P - 1, (UN * GT).bit_length() - 1, ALU.bitwise_and,
                                 ALU.logical_shift_left))
            link(V.tensor_scalar(tmp2_i[:], at_i, shift, UN * GT - 1, ALU.logical_shift_right, ALU.bitwise_and))
            link(V.tensor_tensor(tmp_i[:], tmp_i[:], tmp2_i[:], ALU.bitwise_or))
            link(V.tensor_scalar(tmp2_i[:], at_i, (1 << 24) - turn_edges, None, ALU.bitwise_and))
            V.tensor_tensor(at_i, tmp_i[:], tmp2_i[:], ALU.bitwise_or).then_inc(s_rows, 1)

            def records(c, r, turn, first=False):
                dve.wait_ge(s_hi, c + 1)
                V.tensor_tensor(ea_r[:, r, :, :], ea_in[:, r, :, :], rec[:, r, :, 0:F], ALU.subtract)\
                    .then_inc(s_rest, 1)
                pairs = rec[:, r, :, :].rearrange("l k c -> l (k c)").bitcast(fp32)\
                    .rearrange("l (k c) -> l k c", k=CK)[:, :, KO // 2 + 2:KO // 2 + 4]
                V.tensor_copy(pairs, pair[:, bass.ds(c * CK, CK), :])
                dve.wait_ge(s_mid, c + 1)
                V.tensor_tensor(rec[:, r, :, 5 * F:6 * F], ea_r[:, r, :, :], rec[:, r, :, 3 * F:4 * F], ALU.subtract)\
                    .then_inc(s_rec, 1)

            for r in range(2):
                records(r, r, 0, True)
            dve.wait_ge(s_w, 13 * 16)
            for v, p in ((wc, wpart), (bw, bpart)):
                link(V.tensor_copy(p[:, 0, :], v[:]))
                link(V.tensor_tensor(v[:], v[:], p[:, 0, :], ALU.subtract))
                link(V.tensor_copy(p[:, 1, :], v[:]))
                link(V.tensor_tensor(p[:, 2, :], v[:], p[:, 1, :], ALU.subtract))
            for k in range(4):
                last = V.tensor_tensor(wdiag[:, k, :, :], wrep[:, k, :].unsqueeze(1).to_broadcast([P, 8, F]),
                                       diag.unsqueeze(2).to_broadcast([P, 8, F]), ALU.mult)
            last.then_inc(s_wparts, 1)

            def parts(v):
                t3 = T48[:].rearrange("p (a c) -> p a c", a=NBX)
                v3, r3 = blocks(v[:], NBX), blocks(Pr[:], NBX)
                link(V.tensor_copy(t3[:, :, 0:F], v3))
                link(V.tensor_tensor(r3, v3, t3[:, :, 0:F], ALU.subtract))
                link(V.tensor_copy(t3[:, :, F:2 * F], r3))
                V.tensor_tensor(t3[:, :, 2 * F:], r3, t3[:, :, F:2 * F], ALU.subtract).then_inc(s_tabready, 1)

            dve.wait_ge(s_x, 48)
            parts(X)
            with dve.Fori(1, NC // 2) as c2:
                for r in range(2):
                    records(c2 * 2 + r, r, c2)

            def take(i, r, turn):
                dve.wait_ge(s_ex[r], 16 * (turn + 1))
                v = (er[:].rearrange("p u q c -> p (u q c)"), blank[:].rearrange("p a c -> p (a c)"))[r]
                pairs = v.bitcast(fp32).rearrange("p (t c) -> p c t", t=UN * GT)[:, KO // 2 + 2:KO // 2 + 4, :]
                V.tensor_copy(tab[:, :, bass.ds(i * UN * GT, UN * GT)], pairs).then_inc(s_exd, 1)

            with dve.Fori(0, IT // 2) as i2:
                for r in range(2):
                    take(2 * i2 + r, r, i2)
            if IT % 2:
                take(IT - 1, 0, IT // 2)
            dve.wait_ge(s_exd, IT)
            link(V.tensor_copy(src2_i[:], tab[:, 1, :]))
            link(V.tensor_scalar(sources[:, PAD:PAD + NT], src2_i[0:1, :], shift + 1, None, ALU.logical_shift_right))
            link(V.tensor_scalar(src2_i[:], src2_i[:], 2 * P - 1, None, ALU.bitwise_and))
            link(V.tensor_copy(tab[:, 1, :], src2_i[:]))
            link(V.tensor_copy(dst2_i[:], tab[:, 0, :]))
            link(V.tensor_scalar(dst2_i[:], dst2_i[:], shift, None, ALU.logical_shift_right))
            link(V.tensor_copy(dblk[:], dst2_i[:]))
            V.scalar_tensor_tensor(dblk2[:], dblk[:], float(NB), dblk[:], ALU.is_lt, ALU.mult).then_inc(s_tabs, 1)

            tail = NT - (NCH - 1) * P

            def banks(k):
                return [(W[0], W[1]), (TX, H), (acc[:, 0:512], acc[:, 512:1024]),
                        (acc[:, 1024:1536], acc[:, 1536:2048])][k]

            def each(k):
                b0, b1 = banks(k)
                c = lambda v, m: v[:, 0:m * P].rearrange("p (c e) -> p c e", e=P)
                return [(slice(0, 4), P, c(b0, 4)), (slice(4, NCH - 1), P, c(b1, NCH - 5)),
                        (slice(NCH - 1, NCH), tail, b1[0:tail, (NCH - 5) * P:(NCH - 4) * P].unsqueeze(1))]

            for k, (o, op) in enumerate(((low, ALU.min), (high, ALU.max))):
                dve.wait_ge(s_turn, k + 1)
                for s, r, v in each(k):
                    link(V.tensor_reduce(o[0:r, s], v, AX, op))
            link(V.tensor_tensor(high[:], high[:], low[:], ALU.subtract))
            V.tensor_reduce(span[:], high[:], AX, ALU.max).then_inc(s_low, 1)
            dve.wait_ge(s_turn, 3)
            for s, r, v in each(2):
                last = V.tensor_copy(turned_b[0:r, s, :], v)
            last.then_inc(s_dir, 1)
            dve.wait_ge(s_lows, 32)
            link(V.tensor_reduce(far[:], spans[:], AX, ALU.max))
            link(V.tensor_scalar(far[:], far[:], float(FAST), None, ALU.is_ge))
            link(V.tensor_scalar(near[:], far[:], -1.0, 1.0, ALU.mult, ALU.add))
            link(V.tensor_scalar(lowr[:], lowr[:], near[:, 0:1], None, ALU.mult))
            link(V.scalar_tensor_tensor(rel[:, 0:NT], lowr[:, 0:NT], -float(P), tab[:, 0, :], ALU.mult, ALU.add))
            link(V.tensor_copy(far_i[:], far[0:1, :]))
            link(V.tensor_copy(starts[:, PAD:PAD + NT], lowr[0:1, 0:NT]))
            V.tensor_copy(span[:], far[:]).then_inc(s_rel, 1)
            dve.wait_ge(s_rel, 1)
            dve.wait_ge(s_turn, 4)
            for s, r, v in each(3):
                last = V.tensor_copy(turned_i[0:r, s, :], v)
            last.then_inc(s_dir, 1)

            def turn_places(ph, i, u):
                n = NG * ph + UN * i + u
                dve.wait_ge(s_er[u], loads_done(ph, i))
                if positive(n - 1):
                    dve.wait_ge(s_tx, n - 1)
                V.tensor_scalar(ohT[:, u % 2, 0, :], prow[:, u, :], column[:, 0:1], None, ALU.is_equal)\
                    .then_inc(s_oht, 1)

            def matrices(i, u, b):
                n = NG * 3 + UN * i + u
                dve.wait_ge(s_lin, 2 * n + b + 1)
                dve.wait_ge(s_red, n - UN + 1)
                V.tensor_tensor(wr[:, u, 2 * b:2 * b + 2, :], W[b][:].rearrange("p (q w) -> p q w", q=2),
                                b2r[:].unsqueeze(1).to_broadcast([P, 2, HID]), ALU.add).then_inc(s_wr, 1)

            def sum_in(ph, i, u):
                n = NG * ph + UN * i + u
                dve.wait_ge(s_pprod, n + 1)
                V.tensor_reduce(msg[:, u, :, :], wr[:, u, :, :].rearrange("p q (i o) -> p q o i", o=F), AX, ALU.add)\
                    .then_inc(s_red, 1)

            def windows(ph, i, u):
                n = NG * ph + UN * i + u
                if positive(n - UN + 1):
                    dve.wait_ge(s_scat, n - UN + 1)
                for q in range(GT):
                    t = bass.ds((UN * i + u) * GT + q, 1)
                    last = V.tensor_scalar(oh[:, u, q, :], iota_i[:, 0:FAST * P], rel[:, t], None, ALU.is_equal)
                last.then_inc(s_oh, 1)

            def all_blocks(ph, i, u):
                for q in range(GT):
                    t = (UN * i + u) * GT + q
                    c = NT * BY_DST[ph] + t - 1
                    if positive(c):
                        dve.wait_ge(s_gsc, c)
                    V.tensor_scalar(ohg[:, q % 2, :], iota_i[:], rel[:, bass.ds(t, 1)], None, ALU.is_equal)\
                        .then_inc(s_ohg, 1)

            def step(ph, i, u, wide):
                if behind(i, u, 0):
                    turn_places(ph, i, u)
                if ph < 3 and behind(i, u, 3):
                    if not wide:
                        windows(ph, *behind(i, u, 3))
                    sum_in(ph, *behind(i, u, 3))
                if ph == 3:
                    if behind(i, u, 2):
                        matrices(*behind(i, u, 2), 0)
                    if behind(i, u, 3):
                        sum_in(ph, *behind(i, u, 3))
                    if behind(i, u, 2):
                        matrices(*behind(i, u, 2), 1)
                if behind(i, u, 4):
                    j, v = behind(i, u, 4)
                    dve.wait_ge(s_mhi, NG * ph + UN * j + v + 1)
                    V.tensor_tensor(rest[:, v, :, :], msg[:, v, :, :], m48[:, v, :, 0:F], ALU.subtract)\
                        .then_inc(s_r1, 1)
                if ph == 3 and not wide and behind(i, u, 3):
                    windows(ph, *behind(i, u, 3))
                if behind(i, u, 5):
                    j, v = behind(i, u, 5)
                    dve.wait_ge(s_mmid, NG * ph + UN * j + v + 1)
                    V.tensor_tensor(m48[:, v, :, 2 * F:3 * F], rest[:, v, :, :], m48[:, v, :, F:2 * F], ALU.subtract)\
                        .then_inc(s_lo, 1)
                    if wide:
                        all_blocks(ph, j, v)

            def by_destination(i, u, wide):
                m = UN * i + u
                n = NG * 4 + m
                dve.wait_ge(s_er[u], loads_done(4, i))
                if not wide:
                    dve.wait_ge(s_tx, n - 1)
                    for j in range(FAST):
                        last = V.tensor_scalar(ohT[:, u % 2, j, :], rrow[:, u, :], column[:, j:j + 1], None, ALU.is_equal)
                    last.then_inc(s_oht, 1)
                else:
                    for j in range(NB):
                        if j == 0:
                            dve.wait_ge(s_tx, n)
                        if j > 1:
                            dve.wait_ge(s_yx, (NB - 1) * m + j - 1)
                        last = V.tensor_scalar(ohT[:, 0, j % 2, :], rrow[:, u, :], column[:, j:j + 1], None, ALU.is_equal)
                        last.then_inc(s_yoht if j < NB - 1 else s_oht, 1)
                dve.wait_ge(s_scat, n - UN + 1)
                for q in range(GT):
                    last = V.tensor_scalar(oh[:, u, q, 0:P], iota_i[:, 0:P], tab[:, 1, bass.ds(m * GT + q, 1)], None,
                                           ALU.is_equal)
                last.then_inc(s_ohs, 1)

            def last_phase(i, u, wide):
                turn_places(5, i, u)
                if wide:
                    all_blocks(5, i, u)
                else:
                    windows(5, i, u)

            def norm(v):
                v3, x3, y3 = blocks(v, NB), blocks(X[:], NB), blocks(Z[:], NB)
                link(V.tensor_reduce(st1[:], v3, AX, ALU.add))
                link(V.tensor_scalar(st1[:], st1[:], 1.0 / F, None, ALU.mult))
                link(V.tensor_tensor(x3, v3, over_rows(st1[:]), ALU.subtract))
                link(V.tensor_tensor(y3, x3, x3, ALU.mult))
                link(V.tensor_reduce(st2[:], y3, AX, ALU.add))
                root(V.tensor_scalar(st2[:], st2[:], 1.0 / F, EPS, ALU.mult, ALU.add))
                link(V.reciprocal(st3[:], st3[:]))
                link(V.tensor_tensor(x3, x3, over_rows(st3[:]), ALU.mult))

            def root(ins):
                nvar[0] += 1
                ins.then_inc(s_var, 1)
                dve.wait_ge(s_std, nvar[0])

            def column_mean(k, v):
                link(V.tensor_reduce(col[:], v[:].rearrange("p (a f) -> p f a", f=F), AX, ALU.add))
                V.tensor_copy(col2[:], col[:]).then_inc(s_bnin, 1)
                dve.wait_ge(s_bnout, k)
                link(V.tensor_scalar(col[:], H[:, 0:F], 1.0 / N, None, ALU.mult))

            def nodes(ph):
                dve.wait_ge(s_closed, ph + 1)
                y3 = blocks(Y[:], NB)
                if ph == 0 or ph == 4:
                    k = 1 if ph == 0 else 0
                    link(V.tensor_scalar(cnt[:, k, :], acc3[:, 0:NB, 3 * F], 1.0, None, ALU.max))
                if ph == 0:
                    link(V.reciprocal(icnt[:], cnt[:, 1, :]))
                link(V.tensor_copy(y3, acc3[:, 0:NB, 0:F]))
                link(V.tensor_tensor(y3, y3, acc3[:, 0:NB, F:2 * F], ALU.add))
                link(V.tensor_tensor(y3, y3, acc3[:, 0:NB, 2 * F:3 * F], ALU.add))
                if ph < 3:
                    link(V.tensor_tensor(y3, y3, over_rows(icnt[:]), ALU.mult))
                if ph < 4:
                    dve.wait_ge(s_root, ph + 1)
                    link(V.tensor_tensor(Y[:], Y[:], W[1][:, 0:ACC], ALU.add))
                if ph < 2:
                    link(V.tensor_tensor(blocks(X[:], NB), y3, all_rows(row[:, ph, :]), ALU.add))
                    parts(X)
                elif ph == 2:
                    link(V.tensor_tensor(y3, y3, all_rows(row[:, ph, :]), ALU.add))
                    link(V.tensor_tensor(Y[:], Y[:], X0[:, 0:ACC], ALU.add))
                    norm(Y[:])
                    parts(X)
                elif ph == 3:
                    link(V.tensor_tensor(y3, y3, all_rows(row[:, 3, :]), ALU.add))
                    column_mean(1, Y)
                    link(V.tensor_tensor(y3, y3, all_rows(col[:]), ALU.subtract))
                    link(V.tensor_tensor(Z[:], Y[:], Y[:], ALU.mult))
                    column_mean(2, Z)
                    root(V.tensor_scalar(col2[:], col[:], EPS, None, ALU.add))
                    link(V.reciprocal(col3[:], col3[:]))
                    link(V.tensor_tensor(col3[:], col3[:], row[:, 4, :], ALU.mult))
                    link(V.tensor_tensor(y3, y3, all_rows(col3[:]), ALU.mult))
                    link(V.tensor_tensor(y3, y3, all_rows(row[:, 5, :]), ALU.add))
                    link(V.scalar_tensor_tensor(Y[:], Y[:], 0.0, X[:, 0:ACC], ALU.max, ALU.add))
                    norm(Y[:])
                    V.tensor_copy(st1[:], st2[:]).then_inc(s_yst, 1)
                    dve.wait_ge(s_yrows, 16 * NB)
                    parts(Rr)
                elif ph == 4:
                    link(V.tensor_tensor(Y[:], Y[:], X[:, 0:ACC], ALU.add))
                    norm(Y[:])
                    root(V.tensor_copy(st1[:], st2[:]))
                    link(V.reciprocal(rdeg[:], rdeg[:]))
                    link(V.tensor_tensor(blocks(Rr[:], NB), blocks(X[:], NB), over_rows(rdeg[:, 0, :]), ALU.mult))
                    parts(Rr)
                else:
                    link(V.tensor_tensor(y3, y3, over_rows(rdeg[:, 1, :]), ALU.mult))
                    link(V.tensor_tensor(Y[:], Y[:], X[:, 0:ACC], ALU.add))
                    norm(Y[:])
                    V.tensor_copy(st1[:], st2[:]).then_inc(s_tabready, 1)

            far_v = dve.value_load(far_i[0:1, 0:1], min_val=0, max_val=1)
            for ph in range(6):
                def run(wide):
                    if ph < 4:
                        turns(dve, lambda i, u: step(ph, i, u, wide))
                    else:
                        with dve.Fori(0, IT) as i:
                            for u in range(UN):
                                by_destination(i, u, wide) if ph == 4 else last_phase(i, u, wide)
                with dve.If(far_v < 1):
                    run(False)
                with dve.Else():
                    run(True)
                nodes(ph)

        @block.tensor
        def _(pe):
            T = nc.tensor

            pe.wait_ge(s_cst, 32)
            pe.wait_ge(s_hist, 1)
            T.matmul(W[0][0:LANES, 0:NB], before[0:LANES, 0:LANES], hist[:], start=True, stop=True)
            T.matmul(W[1][0:LANES, 0:NB], ones[0:LANES, 0:LANES], hist[:], start=True, stop=True).then_inc(s_pre, 1)

            def turn(b0, b1, v):
                for c in range(NCH):
                    k = min(P, NT - P * c)
                    b, o = (b0, c) if c < 4 else (b1, c - 4)
                    last = T.transpose(b[0:k, P * o:P * o + P], v[:, P * c:P * c + k], ident)
                last.then_inc(s_turn, 1)

            pe.wait_ge(s_tabs, 1)
            turn(W[0], W[1], dblk[:])
            turn(TX, H, dblk2[:])
            turn(acc[:, 0:512], acc[:, 512:1024], tab[:, 1, :])
            pe.wait_ge(s_rel, 1)
            turn(acc[:, 1024:1536], acc[:, 1536:2048], rel[:, 0:NT])
            pe.wait_ge(s_dir, 2)
            pe.wait_ge(s_const, 1)
            pe.wait_ge(s_wparts, 1)
            pe.wait_ge(s_wstack, 16 * (len(WSTACK) + PIECES))
            far_v = pe.value_load(far_i[0:1, 0:1], min_val=0, max_val=1)

            def blocks_of(table, i, lag):
                tiles = bass.ds(UN * GT * i + PAD - GT * lag, UN * GT)
                return nc.values_load_multi_w_load_instructions(
                    table[0:1, tiles], engines=[mybir.EngineType.PE], min_val=0, max_val=NB,
                    skip_runtime_bounds_check_because="blocks are numbered below that")[1]

            def addresses(aps):
                for ap in aps:
                    pe.lower_ap(ap)
                return aps

            def open_acc(stop):
                for b in range(4):
                    last = T.matmul(acc[:, 512 * b:512 * b + 512], zeros[:, 0:P], zeros[:], start=not stop, stop=stop,
                                    skip_group_check=True)
                return last

            def rows_in(ph, i, u, source):
                n = NG * ph + UN * i + u
                k = PIECES * F
                tables = addresses([T48[:, bass.ds(source[GT * u + q] * k, k)] for q in range(GT)])
                pe.wait_ge(s_er[u], loads_done(ph, i))
                if positive(n):
                    pe.wait_ge(s_txc, n)
                if ph < 4:
                    for q in range(GT):
                        T.transpose(t_out[0:REC, P * q:P * q + P], er[:, u, q, :], identb[:])
                pe.wait_ge(s_oht, n + 1)
                for q in range(GT):
                    last = T.matmul(x_out(k)[:, k * q:k * q + k], ohT[:, u % 2, 0, P * q:P * q + P], tables[q],
                                    start=True, stop=True)
                last.then_inc(s_tx, 1)

            def rows_by_destination(i, u, wide, start):
                m, k = UN * i + u, PIECES * F
                n = NG * 4 + m
                pe.wait_ge(s_txc, n)
                if not wide:
                    tables = addresses([T48[:, bass.ds(start[GT * u + q] * k + k * j, k)]
                                        for q in range(GT) for j in range(FAST)])
                    pe.wait_ge(s_oht, n + 1)
                    for q in range(GT):
                        for j in range(FAST):
                            last = T.matmul(x_out(k)[:, k * q:k * q + k], ohT[:, u % 2, j, P * q:P * q + P],
                                            tables[FAST * q + j], start=(j == 0), stop=(j == FAST - 1))
                else:
                    for j in range(NB):
                        if j < NB - 1:
                            pe.wait_ge(s_yoht, (NB - 1) * m + j + 1)
                        else:
                            pe.wait_ge(s_oht, n + 1)
                        for q in range(GT):
                            last = T.matmul(x_out(k)[:, k * q:k * q + k], ohT[:, 0, j % 2, P * q:P * q + P],
                                            T48[:, k * j:k * j + k], start=(j == 0 and q == 0), stop=(j == NB - 1),
                                            skip_group_check=True)
                        if j < NB - 1:
                            last.then_inc(s_yx, 1)
                last.then_inc(s_tx, 1)

            def linear(ph, i, u):
                n = NG * ph + UN * i + u
                pe.wait_ge(s_txc, n + 1)
                for q in range(GT):
                    if q % 2 == 0 and positive(n):
                        pe.wait_ge(s_wr, 2 * (n - 1) + q // 2 + 1)
                    last = T.matmul(W[q // 2][:, HID * (q % 2):HID * (q % 2) + HID],
                                    eT[0:KS, u % 2, P * q:P * q + P], wstack[:, HID * ph:HID * ph + HID],
                                    start=True, stop=True)
                    if q % 2:
                        last.then_inc(s_lin, 1)

            def hidden(i, u, h):
                n, m = NG * 3 + UN * i + u, UN * i + u
                if h == 0:
                    pe.wait_ge(s_txc, n + 1)
                if positive(2 * m + h):
                    pe.wait_ge(s_relu, 2 * m + h)
                T.matmul(H[:], wstack[:, HID * 3 + P * h:HID * 3 + P * h + P], eT[0:KS, u % 2, :],
                         start=True, stop=True).then_inc(s_h, 1)

            def second(i, u, q):
                n, m = NG * 3 + UN * i + u, UN * i + u
                o = W[q // 2][:, HID * (q % 2):HID * (q % 2) + HID]
                if q == 0:
                    pe.wait_ge(s_relu, 2 * m + 2)
                if q % 2 == 0:
                    pe.wait_ge(s_wr, 2 * (n - 1) + q // 2 + 1)
                for k in range(2):
                    last = T.matmul(o, hs[:, u % 2, k, P * q:P * q + P], w2s[:, k, :], start=(k == 0), stop=(k == 1))
                if q % 2:
                    last.then_inc(s_lin, 1)

            def scatter(ph, i, u, wide, start):
                m = UN * i + u
                n = NG * ph + m
                if ph < 4:
                    pe.wait_ge(s_lo, n + 1)
                else:
                    pe.wait_ge(s_txc, n + 1)
                if ph == 4:
                    pe.wait_ge(s_ohs, m + 1)
                elif not wide:
                    pe.wait_ge(s_oh, NG * BY_DST[ph] + m + 1)
                if ph == 4:
                    sums = addresses([acc[:, bass.ds(start[q] * SLOT, 3 * F + 1)] for q in range(GT)])
                elif not wide:
                    sums = addresses([acc[:, bass.ds(start[q] * SLOT + SLOT * j, 3 * F + 1)]
                                      for q in range(GT) for j in range(FAST)])
                for q in range(GT):
                    x = m48[:, u, q, 0:3 * F + 1]
                    if ph == 4:
                        last = T.matmul(sums[q], oh[:, u, q, 0:P], x,
                                        start=False, stop=False, skip_group_check=True)
                    elif not wide:
                        for j in range(FAST):
                            last = T.matmul(sums[FAST * q + j], oh[:, u, q, P * j:P * j + P], x, start=False, stop=False,
                                            skip_group_check=True)
                    else:
                        pe.wait_ge(s_ohg, NT * BY_DST[ph] + m * GT + q + 1)
                        for j in range(NB):
                            last = T.matmul(acc[:, SLOT * j:SLOT * j + 3 * F + 1], ohg[:, q % 2, P * j:P * j + P], x,
                                            start=False, stop=False, skip_group_check=True)
                        if q < GT - 1:
                            last.then_inc(s_gsc, 1)
                        else:
                            last.then_inc(s_gsc, 1)
                            last = T.matmul(acc[:, 0:P], zeros[:, 0:P], zeros[:, 0:P], start=False, stop=False,
                                            skip_group_check=True)
                last.then_inc(s_scat, 1)

            def run(ph, wide):
                lag = {True: LAG - 1, False: LAG}[wide] if ph < 4 else 0 if ph == 5 and wide else 2
                gathered = starts if ph == 4 else sources
                scattered = sources if ph == 4 else starts
                regs = [None, None]

                def step(i, u):
                    if u == 0:
                        if not (ph == 4 and wide) and behind(i, 0, 0):
                            regs[0] = blocks_of(gathered, i, 0)
                        if (ph == 4 or not wide) and (behind(i, 0, lag) or behind(i, UN - 1, lag)):
                            regs[1] = blocks_of(scattered, i, lag)
                    if behind(i, u, 0):
                        if ph == 4:
                            rows_by_destination(i, u, wide, regs[0])
                        else:
                            rows_in(ph, i, u, regs[0])
                    before = behind(i, u, 1)
                    if ph < 3 and before:
                        linear(ph, *before)
                    if ph == 3:
                        for q in range(GT):
                            if q >= 2 and behind(i, u, 0):
                                hidden(i, u, q - 2)
                            if before:
                                second(*before, q)
                    if behind(i, u, lag):
                        start = None if wide and ph != 4 else regs[1][GT * u:GT * u + GT]
                        scatter(ph, *behind(i, u, lag), wide, start)

                turns(pe, step)

            for ph in range(6):
                pe.wait_ge(s_tabready, ph + 1)
                open_acc(False)
                with pe.If(far_v < 1):
                    run(ph, False)
                with pe.Else():
                    run(ph, True)
                open_acc(True).then_inc(s_closed, 1)
                if ph < 4:
                    pe.wait_ge(s_wr, 2 * NG * (ph + 1))
                    for c in range(4):
                        k = min(P, ACC - P * c)
                        last = T.transpose(W[0][0:k, P * c:P * c + P], X[:, P * c:P * c + k], ident)
                    last.then_inc(s_ntr, 1)
                    pe.wait_ge(s_ntc, ph + 1)
                    for c in range(4):
                        k = min(P, ACC - P * c)
                        r = wdiag[:, ph, :, :].rearrange("p a f -> p (a f)")[0:k, 0:k]
                        last = T.matmul(W[1][:, P * c:P * c + k], xnt[0:k, P * c:P * c + P], r,
                                        start=True, stop=True)
                    last.then_inc(s_root, 1)
                if ph == 3:
                    for k in range(2):
                        pe.wait_ge(s_bnin, k + 1)
                        T.matmul(H[:, 0:F], live, col2[:], start=True, stop=True).then_inc(s_bnout, 1)


def kernel(**a):
    import numpy as np
    import concourse.bacc as bacc
    from concourse import mybir as mb
    from concourse.bass_utils import run_bass_kernel_spmd as run

    a = {k: np.asarray(v) for k, v in a.items()}
    names = [f"L0_gnn_Wn{k}" for k in (1, 2, 3)] + ["L1_gnn_W1"]
    biases = [f"L0_gnn_bn{k}" for k in (1, 2, 3)] + ["L1_gnn_b1", "L1_gnn_b2"]
    roots = [f"L0_gnn_Wr{k}" for k in (1, 2, 3)] + ["L1_gnn_root"]
    lines = [f"L0_gnn_b{k}" for k in (1, 2, 3)] + ["L1_gnn_bias", "L1_gnn_gamma", "L1_gnn_beta"]
    place = np.arange(P)
    consts = np.zeros((P, CW), np.float32)
    consts[:, 0:P] = np.eye(P)
    consts[:BN, P:2 * P] = 1
    consts[:, 2 * P:3 * P] = place[:, None] < place
    consts[:, 3 * P:4 * P] = place
    consts[:, 4 * P:4 * P + NB] = place[:, None] + P * np.arange(NB)
    consts[:, 4 * P + NB:4 * P + NB + 8] = place[:, None] // F == np.arange(8)
    arrays = {
        "x": a["x"],
        "src": a["src"].reshape(LANES, PER),
        "dst": a["dst"].reshape(LANES, PER),
        "dst_n": a["dst"][:N].reshape(NB, BN).T,
        "ea": a["edge_attr_16"].reshape(LANES, PER * F),
        "wcat": np.concatenate([a[k] for k in names], axis=1),
        "bias3": np.concatenate([a[k] for k in biases])[None, :],
        "rows": np.concatenate([a[k] for k in lines])[None, :],
        "wroot": np.stack([a[k] for k in roots], axis=1),
        "w2": a["L1_gnn_W2"],
        "consts": consts,
        "iota_h": np.arange(NB * P, dtype=np.int16)[None, :],
    }
    arrays = {f"in_{k}": np.ascontiguousarray(v) for k, v in arrays.items()}
    nc = bacc.Bacc("TRN2", target_bir_lowering=False, num_devices=1)
    args = [nc.dram_tensor(k, v.shape, mb.dt.from_np(v.dtype), kind="ExternalInput").ap() for k, v in arrays.items()]
    out = nc.dram_tensor("out_x", (N, F), mb.dt.float32, kind="ExternalOutput").ap()
    gnn_kernel(nc, *args, out)
    return run(nc, [arrays], core_ids=[0]).results[0]["out_x"]
```

```python
import concourse.bass as bass
from concourse import mybir
from contextlib import ExitStack

N = 3125
E = 100000
F = 16
HID = F * F
P = 128
PIECES = 3
GT = 4
GE = GT * P
UN = 4
NB = -(-N // P)
BN = N // NB
assert BN * NB == N
DSHIFT = 19
DMUL = -(-(1 << DSHIFT) // BN)
assert all(k * DMUL >> DSHIFT == k // BN for k in range(N)) and N * DMUL < 1 << 24
LANES = next(k for k in range(P, 0, -1) if E % k == 0)
PER = E // LANES
NG = -(-((E + NB * (P - 1)) // P) // (UN * GT)) * UN
NT = NG * GT
IT = NG // UN
ACC = NB * F
NBX = 32
SLOT = 64
FAST = 3
KEY = 2 * P
BANK = 512
HOMES = 8
STACK = (0, 0, 0, 1, 1, 2)
WSTACK = (0, 1, 2, 0, 1, 0)
KO = len(STACK) * F
KS = KO + PIECES
REC = KO + 8
LAG = UN + 2
PAD = GT * LAG
CK = 20
NC = PER // CK
EMPTY_DST = NB * P
EMPTY_PLACE = 200
EPS = 1e-5
NCH = -(-NT // P)
CW = 4 * P + NB + 8




def gnn_kernel(nc, x, src, dst, dst_n, ea, wcat, bias3, rows, wroot, w2, consts, iota_h, out):
    fp32, bf16, i32, i16 = mybir.dt.float32, mybir.dt.bfloat16, mybir.dt.int32, mybir.dt.int16
    ALU, ACT, AX = mybir.AluOpType, mybir.ActivationFunctionType, mybir.AxisListType.X

    ctx = ExitStack()
    with ctx:
        def sb(name, shape, dt):
            return ctx.enter_context(nc.sbuf_tensor(name, shape, dt))

        def pb(name, banks=1):
            return ctx.enter_context(nc.psum_tensor(name, [P, 512 * banks], fp32))

        def sem(name):
            return ctx.enter_context(nc.semaphore(name))

        rec_d = nc.dram_tensor("rec_d", [NG * GE, REC], bf16).ap()
        place_d = nc.dram_tensor("place_d", [NT, P], bf16).ap()
        dplace_d = nc.dram_tensor("dplace_d", [NT, P], i16).ap()
        key_d = nc.dram_tensor("key_d", [NT, P], i16).ap()
        low_d = nc.dram_tensor("low_d", [NCH, P], fp32).ap()
        span_d = nc.dram_tensor("span_d", [1, P], fp32).ap()
        rows_d = nc.dram_tensor("rows_d", [N, F], fp32).ap()

        cst = sb("cst", [P, CW], fp32)
        ident = cst[:, 0:P]
        live = cst[:, P:2 * P]
        before = cst[:, 2 * P:3 * P]
        iota = cst[:, 3 * P:4 * P]
        column = cst[:, 4 * P:4 * P + NB]
        diag = cst[:, 4 * P + NB:4 * P + NB + 8]
        identb = sb("identb", [P, P], bf16)
        iota_i = sb("iota_i", [P, NB * P], i16)
        iota_k = sb("iota_k", [P, FAST * P], i16)
        ones = sb("ones", [P, P], fp32)
        zeros = sb("zeros", [P, 512], bf16)
        wc = sb("wc", [F, 4 * HID], fp32)
        wpart = sb("wpart", [F, PIECES, 4 * HID], bf16)
        bw = sb("bw", [1, 4 * HID], fp32)
        bpart = sb("bpart", [1, PIECES, 4 * HID], bf16)
        b2r = sb("b2r", [P, HID], fp32)
        wstack = sb("wstack", [KS, 4 * HID], bf16)
        row = sb("row", [P, 6, F], fp32)
        wrep = sb("wrep", [P, 4, F], fp32)
        wdiag = sb("wdiag", [P, 4, 8, F], fp32)
        w2s = sb("w2s", [P, 2, HID], fp32)

        ints = sb("ints", [P, 4 * PER], i32)
        src_i, dst_i, tmp_i, tmp2_i = (ints[0:LANES, PER * k:PER * (k + 1)] for k in range(4))
        dstn_i = sb("dstn_i", [P, NB], i32)
        blk = sb("blk", [LANES, PER], fp32)
        pair = sb("pair", [LANES, PER, 2], fp32)
        work = sb("work", [P, NB * PER], bf16)
        same = work[0:LANES, 0:NB * PER].rearrange("l (a k) -> l a k", a=NB)
        key = sb("key", [P, NT], fp32)
        count = key[0:LANES, 0:PER]
        dplace = sb("dplace", [P, NT], fp32)
        pos = dplace[0:LANES, 0:PER]
        hist = sb("hist", [LANES, NB], fp32)
        grp = sb("grp", [LANES, NB], fp32)
        grp_i = sb("grp_i", [LANES, NB], i32)
        gend = sb("gend", [LANES, NB], fp32)
        base = sb("base", [LANES, NB], fp32)
        pos_i = sb("pos_i", [LANES, PER + CK], i32)
        zero_i = sb("zero_i", [LANES, CK], i32)
        stage = sb("stage", [LANES, 2, CK], i32)
        ea_in = sb("ea_in", [LANES, 2, CK, F], fp32)
        ea_r = sb("ea_r", [LANES, 2, CK, F], fp32)
        records = sb("records", [P, 2 * CK * REC], bf16)
        rec = records[0:LANES, :].rearrange("l (r k c) -> l r k c", r=2, k=CK)
        blank = sb("blank", [P, UN * GT, REC], bf16)

        tab = sb("tab", [P, 2, NT], fp32)
        dst2_i = ints[:, 0:NT]
        dblk = sb("dblk", [P, NT], fp32)
        dblk2 = sb("dblk2", [P, NT], fp32)
        low = sb("low", [P, NCH], fp32)
        high = sb("high", [P, NCH], fp32)
        span = sb("span", [P, 1], fp32)
        spans = sb("spans", [P, P], fp32)
        far = sb("far", [P, 1], fp32)
        near = sb("near", [P, 1], fp32)
        far_i = sb("far_i", [1, 1], i32)
        lowr = sb("lowr", [P, NCH * P], fp32)
        rel = sb("rel", [P, NT], fp32)
        src2_i = ints[:, NT:2 * NT]
        starts = sb("starts", [1, 2 * PAD + NT], i32)
        sources = sb("sources", [1, 2 * PAD + NT], i32)
        turned_b = sb("turned_b", [P, NCH, P], bf16)
        turned_i = sb("turned_i", [P, 2, NCH, P], i16)
        homes = sb("homes", [1, 2 * PAD + NT], i32)
        bits_i = ints[0:1, 2 * NT:3 * NT]

        er = sb("er", [P, UN, GT, REC], bf16)
        prow = records[:, 0:UN * GE].rearrange("p (r e) -> p r e", r=UN)
        rrow = records[:, UN * GE:2 * UN * GE].bitcast(i16).rearrange("p (r e) -> p r e", r=UN)
        eT = sb("eT", [REC, 2, GE], bf16)
        ohT = sb("ohT", [P, 2, FAST, GE], bf16)
        xparts = sb("xparts", [P, 2, GT, PIECES, F], fp32)
        xg = sb("xg", [P, UN, GT, F], fp32)
        hs = work[:, 0:4 * 2 * GE].bitcast(fp32).rearrange("p (r h e) -> p r h e", r=2, h=2)
        wr = work[:, 8 * GE:24 * GE].bitcast(fp32).rearrange("p (r q w) -> p r q w", r=UN, q=GT)
        msg = sb("msg", [P, UN, GT, F], fp32)
        rest = sb("rest", [P, UN, GT, F], fp32)
        m48 = sb("m48", [P, UN, GT, SLOT], bf16)
        m3 = work[:, 8 * GE:8 * GE + UN * GT * FAST * (3 * F + 2)]\
            .rearrange("p (r q j c) -> p r q j c", r=UN, q=GT, j=FAST)
        oh = work[:, 24 * GE:24 * GE + UN * GT * FAST * P].rearrange("p (r q w) -> p r q w", r=UN, q=GT)
        ohg = ints[:].bitcast(bf16)[:, 0:2 * NB * P].rearrange("p (r w) -> p r w", r=2)

        X = sb("X", [P, NBX * F], fp32)
        X0 = sb("X0", [P, ACC], fp32)
        T48 = sb("T48", [P, NBX * PIECES * F], bf16)
        Rr = sb("Rr", [P, NBX * F], fp32)
        Pr = sb("Pr", [P, NBX * F], fp32)
        Y = sb("Y", [P, ACC], fp32)
        Z = sb("Z", [P, ACC], fp32)
        xnt = sb("xnt", [P, 512], fp32)
        cnt = sb("cnt", [P, 2, NB], fp32)
        icnt = sb("icnt", [P, NB], fp32)
        rdeg = sb("rdeg", [P, 2, NB], fp32)
        st1 = sb("st1", [P, NB], fp32)
        st2 = sb("st2", [P, NB], fp32)
        st3 = sb("st3", [P, NB], fp32)
        col = sb("col", [P, F], fp32)
        col2 = sb("col2", [P, F], fp32)
        col3 = sb("col3", [P, F], fp32)

        W = [pb("W0"), pb("W1")]
        TX = pb("TX")
        H = pb("H")
        acc = pb("acc", 4)
        acc3 = acc[:].rearrange("p (a s) -> p a s", s=SLOT)
        t_out = TX[:, 0:GE // 2].bitcast(bf16)

        def x_out(wide):
            return TX[:, GE // 2:GE // 2 + GT * wide]

        def y_out(u, q, j, n=1):
            k = PIECES * F
            o = (FAST * (q % 2) + j) * k
            return ((TX, H), W)[u % 2][q // 2][:, o:o + n * k]

        def sums_of(ph):
            return 2 if ph < 3 else PIECES

        def home(j):
            return j // HOMES * BANK + j % HOMES * PIECES * F

        s_cst, s_x, s_idx, s_w, s_out = sem("s_cst"), sem("s_x"), sem("s_idx"), sem("s_wload"), sem("s_out")
        s_ein = [sem(f"s_ein{k}") for k in range(2)]
        s_blank, s_fill = sem("s_blank"), sem("s_fill")
        s_hist, s_pre, s_rows = sem("s_hist"), sem("s_pre"), sem("s_rows")
        s_hi, s_rest, s_mid, s_rec = sem("s_hi"), sem("s_rest"), sem("s_mid"), sem("s_rec")
        s_zero, s_stage = sem("s_zero"), sem("s_stage")
        s_sc = [sem(f"s_sc{k}") for k in range(2)]
        s_ex = [sem(f"s_ex{k}") for k in range(2)]
        s_exd = sem("s_exd")
        s_turn, s_low, s_lowd = sem("s_turn"), sem("s_low"), sem("s_lowd")
        s_lows, s_dir, s_dird = sem("s_lows"), sem("s_dir"), sem("s_dird")
        s_wparts, s_wstack = sem("s_wparts"), sem("s_wstack")
        s_dve, s_const, s_tabready = sem("s_dve"), sem("s_const"), sem("s_tabready")
        s_er = [sem(f"s_er{k}") for k in range(UN)]
        s_oht, s_tx, s_txc, s_lin = sem("s_oht"), sem("s_tx"), sem("s_txc"), sem("s_lin")
        s_h, s_relu = sem("s_h"), sem("s_relu")
        s_wr, s_red, s_mhi, s_r1, s_mmid, s_lo = (sem("s_wr"), sem("s_red"), sem("s_mhi"), sem("s_r1"),
                                                    sem("s_mmid"), sem("s_lo"))
        s_xpart, s_xg, s_pprod = sem("s_xpart"), sem("s_xg"), sem("s_pprod")
        s_oh, s_scat = sem("s_oh"), sem("s_scat")
        s_ohg, s_gsc = sem("s_ohg"), sem("s_gsc")
        s_yoht, s_yx = sem("s_yoht"), sem("s_yx")
        s_ntr, s_ntc, s_root = sem("s_ntr"), sem("s_ntc"), sem("s_root")
        s_bnin, s_bnout = sem("s_bnin"), sem("s_bnout")
        s_var, s_std = sem("s_var"), sem("s_std")
        s_yst, s_ygat, s_yrows = sem("s_yst"), sem("s_ygat"), sem("s_yrows")
        s_rel, s_tabs, s_ohs = sem("s_rel"), sem("s_tabs"), sem("s_ohs")
        s_closed = sem("s_closed")
        s_clear = sem("s_clear")

        block = ctx.enter_context(nc.Block())

        def blocks(ap, a):
            return ap.rearrange("p (a f) -> p a f", f=F)[:, 0:a, :]

        def behind(i, u, lag):
            j, v = i + (u - lag) // UN, (u - lag) % UN
            if isinstance(j, int) and not 0 <= j < IT:
                return None
            return j, v

        def positive(v):
            return not isinstance(v, int) or v > 0

        def turns(eng, step):
            first = 2 + IT % 2
            for i in range(first):
                for u in range(UN):
                    step(i, u)
            with eng.Fori(0, (IT - first) // 2) as pair:
                for h in range(2):
                    for u in range(UN):
                        step(pair * 2 + first + h, u)
            for u in range(LAG):
                step(IT + u // UN, u % UN)


        @block.sync
        def _(sp):
            sp.dma_start(src_i[:], src).then_inc(s_idx, 16)
            sp.dma_start(dst_i[:], dst).then_inc(s_idx, 16)
            sp.dma_start(cst[:], consts).then_inc(s_cst, 16)
            sp.dma_start(iota_i[:], iota_h.to_broadcast([P, NB * P])).then_inc(s_cst, 16)
            sp.wait_ge(s_blank, 1)
            turn_recs = rec_d.rearrange("(i p t) c -> i p (t c)", p=P, t=UN * GT)
            group_recs = rec_d.rearrange("(i p u q) c -> i u p (q c)", p=P, u=UN, q=GT)
            with sp.Fori(0, IT) as i:
                sp.dma_start(turn_recs[bass.ds(i, 1), :, :].rearrange("a p c -> (a p) c"),
                             blank[:].rearrange("p q c -> p (q c)")).then_inc(s_fill, 16)
            eav = ea.rearrange("l (c k) -> l c k", k=CK * F)

            def ea_load(c, r, wait=None):
                if wait is not None:
                    sp.wait_ge(s_rec, wait)
                sp.dma_start(ea_in[:, r, :, :].rearrange("l k f -> l (k f)").unsqueeze(1), eav[:, bass.ds(c, 1), :])\
                  .then_inc(s_ein[r], 16)

            for r in range(2):
                ea_load(r, r)
            sp.wait_ge(s_clear, 1)
            sp.dma_start(X[0:BN, 0:ACC], x.rearrange("(a b) f -> b a f", b=BN)).then_inc(s_x, 16)
            sp.dma_start(X0[0:BN, :], x.rearrange("(a b) f -> b a f", b=BN)).then_inc(s_x, 16)
            sp.dma_start(dstn_i[0:BN, :], dst_n).then_inc(s_x, 16)
            sp.dma_start(wc[:], wcat).then_inc(s_w, 16)
            sp.dma_start(bw[:], bias3[:, 0:4 * HID]).then_inc(s_w, 16)
            sp.dma_start(b2r[:], bias3[:, 4 * HID:].to_broadcast([P, HID])).then_inc(s_w, 16)
            sp.dma_start(row[:].rearrange("p k f -> p (k f)"), rows.to_broadcast([P, 6 * F])).then_inc(s_w, 16)
            sp.dma_start(w2s[:], w2.rearrange("(k p) n -> p k n", p=P)).then_inc(s_w, 16)
            for a in range(8):
                sp.dma_start(wrep[F * a:F * a + F, :, :], wroot).then_inc(s_w, 16)
            with sp.Fori(1, NC // 2) as c2:
                for r in range(2):
                    ea_load(c2 * 2 + r, r, c2 * 2 + r - 1)
            sp.wait_ge(s_wparts, 1)
            for k, q in enumerate(WSTACK):
                sp.dma_start(wstack[F * k:F * k + F, :], wpart[:, q, :]).then_inc(s_wstack, 16)
            for q in range(PIECES):
                sp.dma_start(wstack[KO + q:KO + q + 1, :], bpart[:, q, :]).then_inc(s_wstack, 16)
            for r in range(2):
                sp.wait_ge(s_sc[r], 16 * CK * (NC // 2))

            def sorted_turn(i, r):
                sp.dma_start((er[:].rearrange("p u q c -> p (u q c)"), blank[:].rearrange("p a c -> p (a c)"))[r],
                             turn_recs[bass.ds(i, 1), :, :].rearrange("a p c -> (a p) c")).then_inc(s_ex[r], 16)

            for r in range(2):
                sorted_turn(r, r)
            with sp.Fori(1, IT // 2) as i2:
                for r in range(2):
                    sp.wait_ge(s_exd, 2 * i2 + r - 1)
                    sorted_turn(2 * i2 + r, r)
            if IT % 2:
                sp.wait_ge(s_exd, IT - 2)
                sorted_turn(IT - 1, 0)

            def records(u, i, s):
                sp.dma_start(er[:, u, :, :].rearrange("p q c -> p (q c)"),
                             group_recs[bass.ds(i, 1), u, :, :].rearrange("a p c -> (a p) c")).then_inc(s, 16)

            sp.wait_ge(s_low, 1)
            sp.dma_start(low_d.rearrange("c p -> p c"), low[:], allow_slow_non_contiguous=True).then_inc(s_lowd, 16)
            sp.dma_start(span_d.rearrange("a p -> p a"), span[:], allow_slow_non_contiguous=True).then_inc(s_lowd, 16)
            sp.wait_ge(s_lowd, 32)
            sp.dma_start(lowr[:], low_d.rearrange("c p -> (c p)").unsqueeze(0).to_broadcast([P, NCH * P]))\
              .then_inc(s_lows, 16)
            sp.dma_start(spans[:], span_d.to_broadcast([P, P])).then_inc(s_lows, 16)
            for k, (turned, d) in enumerate(((turned_b[:], place_d), (turned_i[:, 0, :, :], dplace_d),
                                             (turned_i[:, 1, :, :], key_d))):
                sp.wait_ge(s_dir, k + 1)
                whole = (NCH - 1) * P
                sp.dma_start(d[0:whole, :].rearrange("(c t) e -> t c e", t=P), turned[:, 0:NCH - 1, :])\
                  .then_inc(s_dird, 16)
                sp.dma_start(d[whole:NT, :], turned[0:NT - whole, NCH - 1, :]).then_inc(s_dird, 16)
            sp.wait_ge(s_dird, 96)
            places = place_d.rearrange("(g q) e -> g (q e)", q=GT)
            dplaces = dplace_d.rearrange("(g q) e -> g (q e)", q=GT)
            keys = key_d.rearrange("(g q) e -> g (q e)", q=GT)

            def load(ph, i, first=False):
                for u in range(UN):
                    n = NG * ph + UN * i + u
                    g = UN * i + u
                    if not first:
                        sp.wait_ge(s_tx, n - UN + 1)
                    if ph < 4:
                        records(u, i, s_er[u])
                    if ph >= 4:
                        rows_of = dplaces if ph == 4 else keys
                        sp.dma_start(rrow[:, u, :], rows_of[bass.ds(g, 1), :].to_broadcast([P, GE])).then_inc(s_er[u], 16)
                    else:
                        sp.dma_start(prow[:, u, :], places[bass.ds(g, 1), :].to_broadcast([P, GE]))\
                          .then_inc(s_er[u], 16)

            for ph in range(6):
                if ph == 4:
                    sp.wait_ge(s_yst, 1)
                    sp.dma_start(rows_d.rearrange("(a b) f -> b a f", b=BN), blocks(X[0:BN, :], NB)).then_inc(s_ygat, 16)
                load(ph, 0, ph == 0)
                with sp.Fori(1, IT) as i:
                    load(ph, i)
            sp.wait_ge(s_tabready, 7)
            sp.dma_start(out.rearrange("(a b) f -> b a f", b=BN), blocks(X[0:BN, :], NB)).then_inc(s_out, 16)
            sp.wait_ge(s_out, 16)

        def loads_done(ph, i):
            before_ph = 32 * IT * min(ph, 4) + 16 * IT * max(ph - 4, 0)
            return before_ph + (32 if ph < 4 else 16) * (i + 1)

        def product(eng, u, a, b):
            w = wr[:, u, a:b, :].rearrange("p q (i o) -> p (q i) o", o=F)
            xi = xg[:, u, a:b, :].rearrange("p q f -> p (q f)").unsqueeze(2).to_broadcast([P, (b - a) * F, F])
            return eng.tensor_tensor(w, w, xi, ALU.mult)

        BY_DST = {0: 0, 1: 1, 2: 2, 3: 3, 5: 4}

        @block.gpsimd
        def _(pool):
            pool.memset(blank[:], 0.0).then_inc(s_zero, 1)
            pool.memset(rec[:], 1.0).then_inc(s_zero, 1)
            pool.memset(zero_i[:], 0).then_inc(s_zero, 1)
            pool.memset(m48[:], 1.0).then_inc(s_zero, 1)
            pool.wait_ge(s_zero, 4)
            blank_f = blank[:].rearrange("p q c -> p (q c)").bitcast(fp32).rearrange("p (q c) -> p q c", q=UN * GT)
            pool.memset(blank_f[:, :, KO // 2 + 2:KO // 2 + 3], float(EMPTY_DST)).then_inc(s_zero, 1)
            pool.wait_ge(s_zero, 5)
            pool.memset(blank_f[:, :, KO // 2 + 3:KO // 2 + 4], float(EMPTY_PLACE)).then_inc(s_blank, 1)
            pool.wait_ge(s_rows, 1)

            HK = CK // 2

            def stage_half(c, r, h):
                pool.tensor_tensor(stage[:, r, HK * h:HK * h + HK], pos_i[:, bass.ds(c * CK + HK * h, HK)],
                                   zero_i[:, 0:HK], ALU.add).then_inc(s_stage, 1)

            def scatter_half(r, h):
                for k in range(HK * h, HK * h + HK):
                    pool.indirect_dma_start(rec_d, bass.IndirectOffsetOnAxis(stage[:, r, k:k + 1], 0),
                                            rec[:, r, k, :], None).then_inc(s_sc[r], 16)

            def scatter_chunks(c2, first=False):
                for r in range(2):
                    c = c2 * 2 + r
                    pool.wait_ge(s_rec, c + 1)
                    pool.wait_ge(s_stage, 2 * c + 1)
                    stage_half(c, r, 1)
                    scatter_half(r, 0)
                    if not (first and r == 0):
                        pool.wait_ge(s_sc[1 - r], 16 * CK * (c2 + r))
                    pool.wait_ge(s_stage, 2 * c + 2)
                    stage_half(c + 1, 1 - r, 0)
                    scatter_half(r, 1)

            pool.wait_ge(s_fill, 16 * IT)
            stage_half(0, 0, 0)
            scatter_chunks(0, True)
            with pool.Fori(1, NC // 2) as c2:
                scatter_chunks(c2)

            def step(ph, i, u):
                if behind(i, u, 0):
                    n = NG * ph + UN * i + u
                    pool.wait_ge(s_txc, n + 1)
                    if positive(n - UN + 1):
                        pool.wait_ge(s_pprod, n - UN + 1)
                    xp = xparts[:, u % 2, :, :, :]
                    pool.tensor_tensor(xg[:, u, :, :], xp[:, :, 0, :], xp[:, :, 1, :], ALU.add)\
                        .then_inc(s_xg if ph < 3 else s_xpart, 1)
                    if ph == 3:
                        pool.wait_ge(s_xpart, n - NG * 3 + 1)
                        pool.tensor_tensor(xg[:, u, :, :], xg[:, u, :, :], xp[:, :, 2, :], ALU.add)\
                            .then_inc(s_xg, 1)
                if behind(i, u, 1):
                    j, v = behind(i, u, 1)
                    n = NG * ph + UN * j + v
                    pool.wait_ge(s_xg, n + 1)
                    for a, b in ((0, 2), (2, GT)):
                        pool.wait_ge(s_wr, 2 * n + a // 2 + 1)
                        last = product(pool, v, a, b)
                    last.then_inc(s_pprod, 1)
            for ph in range(4):
                turns(pool, lambda i, u: step(ph, i, u))
            pool.wait_ge(s_ygat, 16)
            for a in range(NB):
                pool.indirect_dma_start(Rr[0:BN, a * F:a * F + F], None, rows_d,
                                        bass.IndirectOffsetOnAxis(dstn_i[0:BN, a:a + 1], 0)).then_inc(s_yrows, 16)

        @block.scalar
        def _(act):
            act.wait_ge(s_cst, 32)
            nc.scalar.activation(identb[:], ident, ACT.Copy).then_inc(s_const, 1)

            def form_chunk(c, r, turn, first=False):
                act.wait_ge(s_ein[r], 16 * (turn + 1))
                if not first:
                    act.wait_ge(s_sc[r], 16 * CK * turn)
                high = ea_in[:, r, :, :].unsqueeze(2).to_broadcast([LANES, CK, 3, F])
                nc.scalar.activation(rec[:, r, :, 0:3 * F].rearrange("l k (j f) -> l k j f", f=F), high, ACT.Copy)\
                    .then_inc(s_hi, 1)
                act.wait_ge(s_rest, c + 1)
                middle = ea_r[:, r, :, :].unsqueeze(2).to_broadcast([LANES, CK, 2, F])
                nc.scalar.activation(rec[:, r, :, 3 * F:5 * F].rearrange("l k (j f) -> l k j f", f=F), middle,
                                     ACT.Copy).then_inc(s_mid, 1)

            act.wait_ge(s_zero, 2)
            for r in range(2):
                form_chunk(r, r, 0, True)
            with act.Fori(1, NC // 2) as c2:
                for r in range(2):
                    form_chunk(c2 * 2 + r, r, c2)

            def matrices(ph, i, u, b):
                n = NG * ph + UN * i + u
                act.wait_ge(s_lin, 2 * n + b + 1)
                if positive(n - UN + 1):
                    act.wait_ge(s_red, n - UN + 1)
                nc.scalar.activation(wr[:, u, 2 * b:2 * b + 2, :].rearrange("p q w -> p (q w)"), W[b][:],
                                     ACT.Relu).then_inc(s_wr, 1)

            def step(ph, i, u):
                if behind(i, u, 4):
                    j, v = behind(i, u, 4)
                    n = NG * ph + UN * j + v
                    act.wait_ge(s_red, n + 1)
                    if positive(n - UN + 1):
                        act.wait_ge(s_scat, n - UN + 1)
                    nc.scalar.activation(m48[:, v, :, 0:F], msg[:, v, :, :], ACT.Copy).then_inc(s_mhi, 1)
                if behind(i, u, 5):
                    j, v = behind(i, u, 5)
                    n = NG * ph + UN * j + v
                    act.wait_ge(s_r1, n + 1)
                    nc.scalar.activation(m48[:, v, :, F:2 * F], rest[:, v, :, :], ACT.Copy).then_inc(s_mmid, 1)
                if behind(i, u, 0):
                    n = NG * ph + UN * i + u
                    act.wait_ge(s_tx, n + 1)
                    if positive(n - 1):
                        act.wait_ge(s_lin, 2 * (n - 1))
                        act.wait_ge(s_xg, n - 1)
                    nc.scalar.activation(eT[:, u % 2, :], t_out[0:REC, :], ACT.Copy)
                    k = sums_of(ph)
                    nc.scalar.activation(xparts[:, u % 2, :, 0:k, :],
                                         x_out(k * F).rearrange("p (q c f) -> p q c f", q=GT, f=F), ACT.Copy)\
                        .then_inc(s_txc, 1)
                if ph == 3 and behind(i, u, 0):
                    for h in range(2):
                        act.wait_ge(s_h, 2 * (UN * i + u) + h + 1)
                        nc.scalar.activation(hs[:, u % 2, h, :], H[:], ACT.Relu).then_inc(s_relu, 1)
                if ph < 3 and behind(i, u, 1):
                    for b in range(2):
                        matrices(ph, *behind(i, u, 1), b)

            def sqrt(k, r, v):
                act.wait_ge(s_var, k)
                nc.scalar.activation(r, v, ACT.Sqrt).then_inc(s_std, 1)

            act.wait_ge(s_zero, 4)
            for ph in range(4):
                turns(act, lambda i, u: step(ph, i, u))
                act.wait_ge(s_ntr, ph + 1)
                whole = ACC // P * P
                nc.scalar.activation(xnt[:, 0:whole], W[0][:, 0:whole], ACT.Copy)
                nc.scalar.activation(xnt[0:ACC - whole, whole:], W[0][0:ACC - whole, whole:], ACT.Copy)\
                    .then_inc(s_ntc, 1)
                if ph == 2:
                    sqrt(1, st3[:], st2[:])
                if ph == 3:
                    sqrt(2, col3[:], col2[:])
                    sqrt(3, st3[:], st2[:])

            def rows_step(ph, i):
                for u in range(UN):
                    n = NG * ph + UN * i + u
                    act.wait_ge(s_tx, n + 1)
                    act.wait_ge(s_scat, n - UN + 1)
                    for h in range(2):
                        rows = y_out(u, 2 * h, 0, 2 * FAST).rearrange("p (q j c) -> p q j c", q=2, j=FAST)
                        last = nc.scalar.activation(m3[:, u, 2 * h:2 * h + 2, :, 0:PIECES * F], rows, ACT.Copy)
                    last.then_inc(s_txc, 1)

            for ph in (4, 5):
                rows_step(ph, 0)
                with act.Fori(1, IT) as i:
                    rows_step(ph, i)
                if ph == 4:
                    sqrt(4, st3[:], st2[:])
                    sqrt(5, rdeg[:], cnt[:])
            sqrt(6, st3[:], st2[:])

        @block.vector
        def _(dve):
            done = [0]
            nvar = [0]

            def link(ins):
                done[0] += 1
                ins.then_inc(s_dve, 1)
                dve.wait_ge(s_dve, done[0])

            def over_rows(v, n=NB):
                return v.unsqueeze(2).to_broadcast([P, n, F])

            def all_rows(c):
                return c.unsqueeze(1).to_broadcast([P, NB, F])

            V = nc.vector
            V.memset(ones[:], 1.0)
            V.memset(starts[:], 0)
            V.memset(sources[:], 0)
            V.memset(homes[:], 0)
            V.memset(zeros[:], 0.0)
            V.memset(X[:], 0.0)
            V.memset(X0[:], 0.0).then_inc(s_clear, 1)
            V.memset(Rr[:], 0.0)
            V.memset(low[:], 0.0)
            V.memset(high[:], 0.0)
            V.memset(pos_i[:, PER:], 0)
            link(V.memset(pos[:], 0.0))
            dve.wait_ge(s_idx, 32)
            shift = P.bit_length() - 1
            for v in (dst_i, src_i):
                link(V.tensor_scalar(tmp_i[:], v[:], DMUL, None, ALU.mult))
                link(V.tensor_scalar(tmp_i[:], tmp_i[:], DSHIFT, None, ALU.logical_shift_right))
                if v is dst_i:
                    link(V.scalar_tensor_tensor(pair[:, :, 0], tmp_i[:], float(P - BN), v[:], ALU.mult, ALU.add))
            link(V.tensor_copy(blk[:], tmp_i[:]))
            link(V.scalar_tensor_tensor(pair[:, :, 1], tmp_i[:], float(2 * P - BN), src_i[:], ALU.mult, ALU.add))
            for a in range(NB):
                link(V.tensor_scalar(same[:, a, :], blk[:], float(a), None, ALU.is_equal))
                link(V.tensor_tensor_scan(count[:], same[:, a, :], same[:, a, :], 0.0, ALU.add, ALU.max))
                V.tensor_copy(hist[:, a:a + 1], count[:, PER - 1:PER])
                link(V.copy_predicated(pos[:], same[:, a, :].bitcast(i16), count[:]))
            V.tensor_copy(grp[:], hist[:]).then_inc(s_hist, 1)
            dve.wait_ge(s_cst, 32)
            V.tensor_copy(iota_k[:].rearrange("p (j c) -> p j c", c=P),
                          iota_i[:, 0:FAST * KEY].rearrange("p (j c) -> p j c", c=KEY)[:, :, 0:P])
            dve.wait_ge(s_pre, 1)
            link(V.tensor_scalar(grp[:], W[1][0:LANES, 0:NB], float(P - 1), None, ALU.add))
            link(V.tensor_copy(grp_i[:], grp[:]))
            link(V.tensor_scalar(grp_i[:], grp_i[:], shift, None, ALU.logical_shift_right))
            link(V.tensor_copy(grp[:], grp_i[:]))
            link(V.tensor_tensor_scan(gend[:], grp[:], grp[:], 0.0, ALU.add, ALU.max))
            link(V.tensor_tensor(base[:], gend[:], grp[:], ALU.subtract))
            link(V.tensor_scalar(base[:], base[:], float(P), -1.0, ALU.mult, ALU.add))
            link(V.tensor_tensor(base[:], base[:], W[0][0:LANES, 0:NB], ALU.add))
            for a in range(NB):
                link(V.scalar_tensor_tensor(pos[:], same[:, a, :], base[:, a:a + 1], pos[:], ALU.mult, ALU.add))
            at_i = pos_i[:, 0:PER]
            turn_edges = UN * GT * P
            link(V.tensor_copy(at_i, pos[:]))
            link(V.tensor_scalar(tmp_i[:], at_i, P - 1, (UN * GT).bit_length() - 1, ALU.bitwise_and,
                                 ALU.logical_shift_left))
            link(V.tensor_scalar(tmp2_i[:], at_i, shift, UN * GT - 1, ALU.logical_shift_right, ALU.bitwise_and))
            link(V.tensor_tensor(tmp_i[:], tmp_i[:], tmp2_i[:], ALU.bitwise_or))
            link(V.tensor_scalar(tmp2_i[:], at_i, (1 << 24) - turn_edges, None, ALU.bitwise_and))
            V.tensor_tensor(at_i, tmp_i[:], tmp2_i[:], ALU.bitwise_or).then_inc(s_rows, 1)

            def records(c, r, turn, first=False):
                dve.wait_ge(s_hi, c + 1)
                V.tensor_tensor(ea_r[:, r, :, :], ea_in[:, r, :, :], rec[:, r, :, 0:F], ALU.subtract)\
                    .then_inc(s_rest, 1)
                pairs = rec[:, r, :, :].rearrange("l k c -> l (k c)").bitcast(fp32)\
                    .rearrange("l (k c) -> l k c", k=CK)[:, :, KO // 2 + 2:KO // 2 + 4]
                V.tensor_copy(pairs, pair[:, bass.ds(c * CK, CK), :])
                dve.wait_ge(s_mid, c + 1)
                V.tensor_tensor(rec[:, r, :, 5 * F:6 * F], ea_r[:, r, :, :], rec[:, r, :, 3 * F:4 * F], ALU.subtract)\
                    .then_inc(s_rec, 1)

            for r in range(2):
                records(r, r, 0, True)
            dve.wait_ge(s_w, 13 * 16)
            for v, p in ((wc, wpart), (bw, bpart)):
                link(V.tensor_copy(p[:, 0, :], v[:]))
                link(V.tensor_tensor(v[:], v[:], p[:, 0, :], ALU.subtract))
                link(V.tensor_copy(p[:, 1, :], v[:]))
                link(V.tensor_tensor(p[:, 2, :], v[:], p[:, 1, :], ALU.subtract))
            for k in range(4):
                last = V.tensor_tensor(wdiag[:, k, :, :], wrep[:, k, :].unsqueeze(1).to_broadcast([P, 8, F]),
                                       diag.unsqueeze(2).to_broadcast([P, 8, F]), ALU.mult)
            last.then_inc(s_wparts, 1)

            def parts(v):
                t3 = T48[:].rearrange("p (a c) -> p a c", a=NBX)
                v3, r3 = blocks(v[:], NBX), blocks(Pr[:], NBX)
                link(V.tensor_copy(t3[:, :, 0:F], v3))
                link(V.tensor_tensor(r3, v3, t3[:, :, 0:F], ALU.subtract))
                link(V.tensor_copy(t3[:, :, F:2 * F], r3))
                V.tensor_tensor(t3[:, :, 2 * F:], r3, t3[:, :, F:2 * F], ALU.subtract).then_inc(s_tabready, 1)

            dve.wait_ge(s_x, 48)
            parts(X)
            with dve.Fori(1, NC // 2) as c2:
                for r in range(2):
                    records(c2 * 2 + r, r, c2)

            def take(i, r, turn):
                dve.wait_ge(s_ex[r], 16 * (turn + 1))
                v = (er[:].rearrange("p u q c -> p (u q c)"), blank[:].rearrange("p a c -> p (a c)"))[r]
                pairs = v.bitcast(fp32).rearrange("p (t c) -> p c t", t=UN * GT)[:, KO // 2 + 2:KO // 2 + 4, :]
                V.tensor_copy(tab[:, :, bass.ds(i * UN * GT, UN * GT)], pairs).then_inc(s_exd, 1)

            with dve.Fori(0, IT // 2) as i2:
                for r in range(2):
                    take(2 * i2 + r, r, i2)
            if IT % 2:
                take(IT - 1, 0, IT // 2)
            dve.wait_ge(s_exd, IT)
            link(V.tensor_copy(src2_i[:], tab[:, 1, :]))
            link(V.tensor_scalar(sources[:, PAD:PAD + NT], src2_i[0:1, :], shift + 1, None, ALU.logical_shift_right))
            link(V.tensor_scalar(src2_i[:], src2_i[:], 2 * P - 1, None, ALU.bitwise_and))
            link(V.tensor_copy(tab[:, 1, :], src2_i[:]))
            link(V.tensor_copy(dst2_i[:], tab[:, 0, :]))
            link(V.tensor_scalar(dst2_i[:], dst2_i[:], shift, None, ALU.logical_shift_right))
            link(V.tensor_copy(dblk[:], dst2_i[:]))
            V.scalar_tensor_tensor(dblk2[:], dblk[:], float(NB), dblk[:], ALU.is_lt, ALU.mult).then_inc(s_tabs, 1)

            tail = NT - (NCH - 1) * P

            def banks(k):
                return [(W[0], W[1]), (TX, H), (acc[:, 0:512], acc[:, 512:1024]),
                        (acc[:, 1024:1536], acc[:, 1536:2048])][k]

            def each(k):
                b0, b1 = banks(k)
                c = lambda v, m: v[:, 0:m * P].rearrange("p (c e) -> p c e", e=P)
                return [(slice(0, 4), P, c(b0, 4)), (slice(4, NCH - 1), P, c(b1, NCH - 5)),
                        (slice(NCH - 1, NCH), tail, b1[0:tail, (NCH - 5) * P:(NCH - 4) * P].unsqueeze(1))]

            for k, (o, op) in enumerate(((low, ALU.min), (high, ALU.max))):
                dve.wait_ge(s_turn, k + 1)
                for s, r, v in each(k):
                    link(V.tensor_reduce(o[0:r, s], v, AX, op))
            link(V.tensor_tensor(high[:], high[:], low[:], ALU.subtract))
            V.tensor_reduce(span[:], high[:], AX, ALU.max).then_inc(s_low, 1)
            dve.wait_ge(s_turn, 3)
            for s, r, v in each(2):
                last = V.tensor_copy(turned_b[0:r, s, :], v)
            last.then_inc(s_dir, 1)
            dve.wait_ge(s_lows, 32)
            link(V.tensor_reduce(far[:], spans[:], AX, ALU.max))
            link(V.tensor_scalar(far[:], far[:], float(FAST), None, ALU.is_ge))
            link(V.tensor_scalar(near[:], far[:], -1.0, 1.0, ALU.mult, ALU.add))
            link(V.tensor_scalar(lowr[:], lowr[:], near[:, 0:1], None, ALU.mult))
            link(V.scalar_tensor_tensor(rel[:, 0:NT], lowr[:, 0:NT], -float(P), tab[:, 0, :], ALU.mult, ALU.add))
            link(V.tensor_copy(far_i[:], far[0:1, :]))
            link(V.tensor_copy(starts[:, PAD:PAD + NT], lowr[0:1, 0:NT]))
            first, h = starts[:, PAD:PAD + NT], homes[:, PAD:PAD + NT]
            link(V.tensor_scalar(bits_i[:], first, HOMES - 1, None, ALU.bitwise_and))
            link(V.tensor_tensor(h, first, bits_i[:], ALU.subtract))
            link(V.tensor_scalar(h, h, BANK // HOMES, None, ALU.mult))
            link(V.tensor_scalar(bits_i[:], bits_i[:], PIECES * F, None, ALU.mult))
            link(V.tensor_tensor(h, h, bits_i[:], ALU.add))
            link(V.tensor_scalar(dblk[:], dblk[:], near[:, 0:1], None, ALU.mult))
            link(V.scalar_tensor_tensor(dplace[:], dblk[:], -float(P), tab[:, 0, :], ALU.mult, ALU.add))
            link(V.tensor_tensor(key[:], dblk[:], lowr[:, 0:NT], ALU.subtract))
            link(V.scalar_tensor_tensor(key[:], key[:], float(KEY), tab[:, 1, :], ALU.mult, ALU.add))
            V.tensor_copy(span[:], far[:]).then_inc(s_rel, 1)
            dve.wait_ge(s_rel, 1)
            for k in range(2):
                dve.wait_ge(s_turn, 4 + k)
                for s, r, v in each((3, 0)[k]):
                    last = V.tensor_copy(turned_i[0:r, k, s, :], v)
                last.then_inc(s_dir, 1)

            def turn_places(ph, i, u):
                n = NG * ph + UN * i + u
                dve.wait_ge(s_er[u], loads_done(ph, i))
                if positive(n - 1):
                    dve.wait_ge(s_tx, n - 1)
                V.tensor_scalar(ohT[:, u % 2, 0, :], prow[:, u, :], column[:, 0:1], None, ALU.is_equal)\
                    .then_inc(s_oht, 1)

            def matrices(i, u, b):
                n = NG * 3 + UN * i + u
                dve.wait_ge(s_lin, 2 * n + b + 1)
                dve.wait_ge(s_red, n - UN + 1)
                V.tensor_tensor(wr[:, u, 2 * b:2 * b + 2, :], W[b][:].rearrange("p (q w) -> p q w", q=2),
                                b2r[:].unsqueeze(1).to_broadcast([P, 2, HID]), ALU.add).then_inc(s_wr, 1)

            def sum_in(ph, i, u):
                n = NG * ph + UN * i + u
                dve.wait_ge(s_pprod, n + 1)
                V.tensor_reduce(msg[:, u, :, :], wr[:, u, :, :].rearrange("p q (i o) -> p q o i", o=F), AX, ALU.add)\
                    .then_inc(s_red, 1)

            def windows(ph, i, u):
                n = NG * ph + UN * i + u
                if positive(n - UN + 1):
                    dve.wait_ge(s_scat, n - UN + 1)
                for q in range(GT):
                    t = bass.ds((UN * i + u) * GT + q, 1)
                    last = V.tensor_scalar(oh[:, u, q, :], iota_i[:, 0:FAST * P], rel[:, t], None, ALU.is_equal)
                last.then_inc(s_oh, 1)

            def all_blocks(ph, i, u):
                for q in range(GT):
                    t = (UN * i + u) * GT + q
                    c = NT * BY_DST[ph] + t - 1
                    if positive(c):
                        dve.wait_ge(s_gsc, c)
                    V.tensor_scalar(ohg[:, q % 2, :], iota_i[:], rel[:, bass.ds(t, 1)], None, ALU.is_equal)\
                        .then_inc(s_ohg, 1)

            def step(ph, i, u, wide):
                if behind(i, u, 0):
                    turn_places(ph, i, u)
                if ph < 3:
                    if not wide and behind(i, u, 4):
                        windows(ph, *behind(i, u, 4))
                    if behind(i, u, 3):
                        sum_in(ph, *behind(i, u, 3))
                if ph == 3:
                    if behind(i, u, 2):
                        matrices(*behind(i, u, 2), 0)
                    if behind(i, u, 3):
                        sum_in(ph, *behind(i, u, 3))
                    if behind(i, u, 2):
                        matrices(*behind(i, u, 2), 1)
                if behind(i, u, 4):
                    j, v = behind(i, u, 4)
                    dve.wait_ge(s_mhi, NG * ph + UN * j + v + 1)
                    V.tensor_tensor(rest[:, v, :, :], msg[:, v, :, :], m48[:, v, :, 0:F], ALU.subtract)\
                        .then_inc(s_r1, 1)
                if ph == 3 and not wide and behind(i, u, 4):
                    windows(ph, *behind(i, u, 4))
                if behind(i, u, 5):
                    j, v = behind(i, u, 5)
                    dve.wait_ge(s_mmid, NG * ph + UN * j + v + 1)
                    V.tensor_tensor(m48[:, v, :, 2 * F:3 * F], rest[:, v, :, :], m48[:, v, :, F:2 * F], ALU.subtract)\
                        .then_inc(s_lo, 1)
                    if wide:
                        all_blocks(ph, j, v)

            def by_destination(i, u, wide):
                m = UN * i + u
                n = NG * 4 + m
                dve.wait_ge(s_er[u], loads_done(4, i))
                if not wide:
                    dve.wait_ge(s_tx, n - 1)
                    V.tensor_scalar(ohT[:, u % 2, 0, :], rrow[:, u, :], column[:, 0:1], None, ALU.is_equal)\
                        .then_inc(s_oht, 1)
                else:
                    for j in range(NB):
                        if j == 0:
                            dve.wait_ge(s_tx, n)
                        if j > 1:
                            dve.wait_ge(s_yx, (NB - 1) * m + j - 1)
                        last = V.tensor_scalar(ohT[:, 0, j % 2, :], rrow[:, u, :], column[:, j:j + 1], None, ALU.is_equal)
                        last.then_inc(s_yoht if j < NB - 1 else s_oht, 1)
                dve.wait_ge(s_scat, n - UN + 1)
                w = 1 if wide else FAST
                for q in range(GT):
                    last = V.tensor_scalar(oh[:, u, q, 0:w * P], iota_k[:, 0:w * P],
                                           key[:, bass.ds(m * GT + q, 1)], None, ALU.is_equal)
                last.then_inc(s_ohs, 1)

            def last_phase(i, u, wide):
                m = UN * i + u
                n = NG * 5 + m
                dve.wait_ge(s_er[u], loads_done(5, i))
                dve.wait_ge(s_tx, n - 1)
                for j in range(1 if wide else FAST):
                    c = KEY // P * j
                    last = V.tensor_scalar(ohT[:, u % 2, j, :], rrow[:, u, :], column[:, c:c + 1], None, ALU.is_equal)
                last.then_inc(s_oht, 1)
                if wide:
                    all_blocks(5, i, u)
                else:
                    dve.wait_ge(s_scat, n - UN + 1)
                    for q in range(GT):
                        last = V.tensor_scalar(oh[:, u, q, 0:P], iota_i[:, 0:P], dplace[:, bass.ds(m * GT + q, 1)],
                                               None, ALU.is_equal)
                    last.then_inc(s_ohs, 1)

            def norm(v):
                v3, x3, y3 = blocks(v, NB), blocks(X[:], NB), blocks(Z[:], NB)
                link(V.tensor_reduce(st1[:], v3, AX, ALU.add))
                link(V.tensor_scalar(st1[:], st1[:], 1.0 / F, None, ALU.mult))
                link(V.tensor_tensor(x3, v3, over_rows(st1[:]), ALU.subtract))
                link(V.tensor_tensor(y3, x3, x3, ALU.mult))
                link(V.tensor_reduce(st2[:], y3, AX, ALU.add))
                root(V.tensor_scalar(st2[:], st2[:], 1.0 / F, EPS, ALU.mult, ALU.add))
                link(V.reciprocal(st3[:], st3[:]))
                link(V.tensor_tensor(x3, x3, over_rows(st3[:]), ALU.mult))

            def root(ins):
                nvar[0] += 1
                ins.then_inc(s_var, 1)
                dve.wait_ge(s_std, nvar[0])

            def column_mean(k, v):
                link(V.tensor_reduce(col[:], v[:].rearrange("p (a f) -> p f a", f=F), AX, ALU.add))
                V.tensor_copy(col2[:], col[:]).then_inc(s_bnin, 1)
                dve.wait_ge(s_bnout, k)
                link(V.tensor_scalar(col[:], H[:, 0:F], 1.0 / N, None, ALU.mult))

            def nodes(ph):
                dve.wait_ge(s_closed, ph + 1)
                y3 = blocks(Y[:], NB)
                if ph == 0 or ph == 4:
                    k = 1 if ph == 0 else 0
                    link(V.tensor_scalar(cnt[:, k, :], acc3[:, 0:NB, 3 * F], 1.0, None, ALU.max))
                if ph == 0:
                    link(V.reciprocal(icnt[:], cnt[:, 1, :]))
                if ph < 5:
                    link(V.tensor_copy(y3, acc3[:, 0:NB, 0:F]))
                    link(V.tensor_tensor(y3, y3, acc3[:, 0:NB, F:2 * F], ALU.add))
                    link(V.tensor_tensor(y3, y3, acc3[:, 0:NB, 2 * F:3 * F], ALU.add))
                else:
                    k = PIECES * F
                    link(V.memset(Y[:], 0.0))
                    for b in range(-(-NB // HOMES)):
                        for at, a, e in ((0, HOMES * b, HOMES), (HOMES, HOMES * (b + 1), FAST - 1)):
                            e = min(e, NB - a)
                            if e > 0:
                                v = acc[:, BANK * b + at * k:BANK * b + (at + e) * k].rearrange("p (a c) -> p a c", c=k)
                                for c in range(PIECES):
                                    link(V.tensor_tensor(y3[:, a:a + e, :], y3[:, a:a + e, :],
                                                         v[:, :, F * c:F * c + F], ALU.add))
                if ph < 3:
                    link(V.tensor_tensor(y3, y3, over_rows(icnt[:]), ALU.mult))
                if ph < 4:
                    dve.wait_ge(s_root, ph + 1)
                    link(V.tensor_tensor(Y[:], Y[:], W[1][:, 0:ACC], ALU.add))
                if ph < 2:
                    link(V.tensor_tensor(blocks(X[:], NB), y3, all_rows(row[:, ph, :]), ALU.add))
                    parts(X)
                elif ph == 2:
                    link(V.tensor_tensor(y3, y3, all_rows(row[:, ph, :]), ALU.add))
                    link(V.tensor_tensor(Y[:], Y[:], X0[:, 0:ACC], ALU.add))
                    norm(Y[:])
                    parts(X)
                elif ph == 3:
                    link(V.tensor_tensor(y3, y3, all_rows(row[:, 3, :]), ALU.add))
                    column_mean(1, Y)
                    link(V.tensor_tensor(y3, y3, all_rows(col[:]), ALU.subtract))
                    link(V.tensor_tensor(Z[:], Y[:], Y[:], ALU.mult))
                    column_mean(2, Z)
                    root(V.tensor_scalar(col2[:], col[:], EPS, None, ALU.add))
                    link(V.reciprocal(col3[:], col3[:]))
                    link(V.tensor_tensor(col3[:], col3[:], row[:, 4, :], ALU.mult))
                    link(V.tensor_tensor(y3, y3, all_rows(col3[:]), ALU.mult))
                    link(V.tensor_tensor(y3, y3, all_rows(row[:, 5, :]), ALU.add))
                    link(V.scalar_tensor_tensor(Y[:], Y[:], 0.0, X[:, 0:ACC], ALU.max, ALU.add))
                    norm(Y[:])
                    V.tensor_copy(st1[:], st2[:]).then_inc(s_yst, 1)
                    V.memset(m3[:], 1.0)
                    dve.wait_ge(s_yrows, 16 * NB)
                    parts(Rr)
                elif ph == 4:
                    link(V.tensor_tensor(Y[:], Y[:], X[:, 0:ACC], ALU.add))
                    norm(Y[:])
                    root(V.tensor_copy(st1[:], st2[:]))
                    link(V.reciprocal(rdeg[:], rdeg[:]))
                    link(V.tensor_tensor(blocks(Rr[:], NB), blocks(X[:], NB), over_rows(rdeg[:, 0, :]), ALU.mult))
                    parts(Rr)
                else:
                    link(V.tensor_tensor(y3, y3, over_rows(rdeg[:, 1, :]), ALU.mult))
                    link(V.tensor_tensor(Y[:], Y[:], X[:, 0:ACC], ALU.add))
                    norm(Y[:])
                    V.tensor_copy(st1[:], st2[:]).then_inc(s_tabready, 1)

            far_v = dve.value_load(far_i[0:1, 0:1], min_val=0, max_val=1)
            for ph in range(6):
                def run(wide):
                    if ph < 4:
                        turns(dve, lambda i, u: step(ph, i, u, wide))
                    else:
                        def turn(i):
                            for u in range(UN):
                                by_destination(i, u, wide) if ph == 4 else last_phase(i, u, wide)

                        with dve.Fori(0, IT // 2) as pair:
                            for h in range(2):
                                turn(pair * 2 + h)
                        for i in range(IT // 2 * 2, IT):
                            turn(i)
                with dve.If(far_v < 1):
                    run(False)
                with dve.Else():
                    run(True)
                nodes(ph)

        @block.tensor
        def _(pe):
            T = nc.tensor

            pe.wait_ge(s_cst, 32)
            pe.wait_ge(s_hist, 1)
            T.matmul(W[0][0:LANES, 0:NB], before[0:LANES, 0:LANES], hist[:], start=True, stop=True)
            T.matmul(W[1][0:LANES, 0:NB], ones[0:LANES, 0:LANES], hist[:], start=True, stop=True).then_inc(s_pre, 1)

            def turn(b0, b1, v):
                for c in range(NCH):
                    k = min(P, NT - P * c)
                    b, o = (b0, c) if c < 4 else (b1, c - 4)
                    last = T.transpose(b[0:k, P * o:P * o + P], v[:, P * c:P * c + k], ident)
                last.then_inc(s_turn, 1)

            pe.wait_ge(s_tabs, 1)
            turn(W[0], W[1], dblk[:])
            turn(TX, H, dblk2[:])
            turn(acc[:, 0:512], acc[:, 512:1024], tab[:, 1, :])
            pe.wait_ge(s_rel, 1)
            turn(acc[:, 1024:1536], acc[:, 1536:2048], dplace[:])
            turn(W[0], W[1], key[:])
            pe.wait_ge(s_dir, 3)
            pe.wait_ge(s_const, 1)
            pe.wait_ge(s_wparts, 1)
            pe.wait_ge(s_wstack, 16 * (len(WSTACK) + PIECES))
            far_v = pe.value_load(far_i[0:1, 0:1], min_val=0, max_val=1)

            def blocks_of(table, i, lag, top=NB):
                tiles = bass.ds(UN * GT * i + PAD - GT * lag, UN * GT)
                return nc.values_load_multi_w_load_instructions(
                    table[0:1, tiles], engines=[mybir.EngineType.PE], min_val=0, max_val=top,
                    skip_runtime_bounds_check_because="blocks are numbered below that")[1]

            def addresses(aps):
                for ap in aps:
                    pe.lower_ap(ap)
                return aps

            def open_acc(stop):
                for b in range(4):
                    last = T.matmul(acc[:, 512 * b:512 * b + 512], zeros[:, 0:P], zeros[:], start=not stop, stop=stop,
                                    skip_group_check=True)
                return last

            def rows_in(ph, i, u, source, wide):
                n = NG * ph + UN * i + u
                k = F * sums_of(ph)
                tables = addresses([T48[:, bass.ds(source[GT * u + q] * (PIECES * F) + c, w)]
                                    for c, w in ((0, k), (k, F))[:1 + (ph < 3)] for q in range(GT)])
                pe.wait_ge(s_er[u], loads_done(ph, i))
                if positive(n):
                    pe.wait_ge(s_txc, n if ph < 4 else n - 1)
                if ph < 4:
                    for q in range(GT):
                        T.transpose(t_out[0:REC, P * q:P * q + P], er[:, u, q, :], identb[:])
                pe.wait_ge(s_oht, n + 1)
                for q in range(GT):
                    if ph < 4:
                        last = T.matmul(x_out(k)[:, k * q:k * q + k], ohT[:, u % 2, 0, P * q:P * q + P], tables[q],
                                        start=True, stop=True)
                        if ph < 3:
                            last = T.matmul(x_out(k)[:, k * q:k * q + F], ohT[:, u % 2, 0, P * q:P * q + P],
                                            tables[GT + q], start=False, stop=True, skip_group_check=True)
                    else:
                        for j in range(1 if wide else FAST):
                            last = T.matmul(y_out(u, q, j), ohT[:, u % 2, j, P * q:P * q + P], tables[q],
                                            start=True, stop=True)
                last.then_inc(s_tx, 1)

            def rows_by_destination(i, u, wide, start):
                m, k = UN * i + u, PIECES * F
                n = NG * 4 + m
                pe.wait_ge(s_txc, n - 1)
                if not wide:
                    tables = addresses([T48[:, bass.ds(start[GT * u + q] * k, FAST * k)] for q in range(GT)])
                    pe.wait_ge(s_oht, n + 1)
                    for q in range(GT):
                        last = T.matmul(y_out(u, q, 0, FAST), ohT[:, u % 2, 0, P * q:P * q + P], tables[q],
                                        start=True, stop=True)
                else:
                    for j in range(NB):
                        if j < NB - 1:
                            pe.wait_ge(s_yoht, (NB - 1) * m + j + 1)
                        else:
                            pe.wait_ge(s_oht, n + 1)
                        for q in range(GT):
                            last = T.matmul(y_out(u, q, 0), ohT[:, 0, j % 2, P * q:P * q + P],
                                            T48[:, k * j:k * j + k], start=(j == 0 and q % 2 == 0),
                                            stop=(j == NB - 1), skip_group_check=True)
                        if j < NB - 1:
                            last.then_inc(s_yx, 1)
                last.then_inc(s_tx, 1)

            def linear(ph, i, u):
                n = NG * ph + UN * i + u
                pe.wait_ge(s_txc, n + 1)
                for q in range(GT):
                    if q % 2 == 0 and positive(n):
                        pe.wait_ge(s_wr, 2 * (n - 1) + q // 2 + 1)
                    last = T.matmul(W[q // 2][:, HID * (q % 2):HID * (q % 2) + HID],
                                    eT[0:KS, u % 2, P * q:P * q + P], wstack[:, HID * ph:HID * ph + HID],
                                    start=True, stop=True)
                    if q % 2:
                        last.then_inc(s_lin, 1)

            def hidden(i, u, h):
                n, m = NG * 3 + UN * i + u, UN * i + u
                if h == 0:
                    pe.wait_ge(s_txc, n + 1)
                if positive(2 * m + h):
                    pe.wait_ge(s_relu, 2 * m + h)
                T.matmul(H[:], wstack[:, HID * 3 + P * h:HID * 3 + P * h + P], eT[0:KS, u % 2, :],
                         start=True, stop=True).then_inc(s_h, 1)

            def second(i, u, q):
                n, m = NG * 3 + UN * i + u, UN * i + u
                o = W[q // 2][:, HID * (q % 2):HID * (q % 2) + HID]
                if q == 0:
                    pe.wait_ge(s_relu, 2 * m + 2)
                if q % 2 == 0:
                    pe.wait_ge(s_wr, 2 * (n - 1) + q // 2 + 1)
                for k in range(2):
                    last = T.matmul(o, hs[:, u % 2, k, P * q:P * q + P], w2s[:, k, :], start=(k == 0), stop=(k == 1))
                if q % 2:
                    last.then_inc(s_lin, 1)

            def scatter(ph, i, u, wide, start):
                m = UN * i + u
                n = NG * ph + m
                if ph < 4:
                    pe.wait_ge(s_lo, n + 1)
                else:
                    pe.wait_ge(s_txc, n + 1)
                if ph >= 4 and not (wide and ph == 5):
                    pe.wait_ge(s_ohs, m + 1 + (NG if ph == 5 and not wide else 0))
                elif not wide:
                    pe.wait_ge(s_oh, n + 1)
                k = PIECES * F
                if ph == 4:
                    sums = addresses([acc[:, bass.ds(start[q] * SLOT, k + 1)] for q in range(GT)])
                elif ph == 5 and not wide:
                    sums = addresses([acc[:, bass.ds(start[q], FAST * k)] for q in range(GT)])
                elif not wide:
                    sums = addresses([acc[:, bass.ds(start[q] * SLOT + SLOT * j, k + 1)]
                                      for q in range(GT) for j in range(FAST)])

                def add(out, one_hots, x):
                    return T.matmul(out, one_hots, x, start=False, stop=False, skip_group_check=True)

                for q in range(GT):
                    if ph == 4:
                        for j in range(1 if wide else FAST):
                            last = add(sums[q], oh[:, u, q, P * j:P * j + P], m3[:, u, q, j, 0:k + 1])
                    elif ph == 5 and not wide:
                        last = add(sums[q], oh[:, u, q, 0:P], m3[:, u, q, :, 0:k])
                    elif not wide:
                        for j in range(FAST):
                            last = add(sums[FAST * q + j], oh[:, u, q, P * j:P * j + P], m48[:, u, q, 0:k + 1])
                    else:
                        pe.wait_ge(s_ohg, NT * BY_DST[ph] + m * GT + q + 1)
                        for j in range(NB):
                            out, x = ((acc[:, SLOT * j:SLOT * j + k + 1], m48[:, u, q, 0:k + 1]) if ph < 4 else
                                      (acc[:, home(j):home(j) + k], m3[:, u, q, 0, 0:k]))
                            last = add(out, ohg[:, q % 2, P * j:P * j + P], x)
                        last.then_inc(s_gsc, 1)
                        if q == GT - 1:
                            last = T.matmul(acc[:, 0:P], zeros[:, 0:P], zeros[:, 0:P], start=False, stop=False,
                                            skip_group_check=True)
                last.then_inc(s_scat, 1)

            def run(ph, wide):
                lag = {True: LAG - 1, False: LAG}[wide] if ph < 4 else 0 if ph == 5 and wide else 2
                gathered = starts if ph == 4 else sources
                scattered = {4: sources, 5: homes}.get(ph, starts)
                regs = [None, None]

                def step(i, u):
                    if u == 0:
                        if not (ph == 4 and wide) and behind(i, 0, 0):
                            regs[0] = blocks_of(gathered, i, 0)
                        if (ph == 4 or not wide) and (behind(i, 0, lag) or behind(i, UN - 1, lag)):
                            regs[1] = blocks_of(scattered, i, lag, home(NB) if ph == 5 else NB)
                    if behind(i, u, 0):
                        if ph == 4:
                            rows_by_destination(i, u, wide, regs[0])
                        else:
                            rows_in(ph, i, u, regs[0], wide)
                    before = behind(i, u, 1)
                    if ph < 3 and before:
                        linear(ph, *before)
                    if ph == 3:
                        for q in range(GT):
                            if q >= 2 and behind(i, u, 0):
                                hidden(i, u, q - 2)
                            if before:
                                second(*before, q)
                    if behind(i, u, lag):
                        start = None if wide and ph != 4 else regs[1][GT * u:GT * u + GT]
                        scatter(ph, *behind(i, u, lag), wide, start)

                turns(pe, step)

            for ph in range(6):
                pe.wait_ge(s_tabready, ph + 1)
                open_acc(False)
                with pe.If(far_v < 1):
                    run(ph, False)
                with pe.Else():
                    run(ph, True)
                open_acc(True).then_inc(s_closed, 1)
                if ph < 4:
                    pe.wait_ge(s_wr, 2 * NG * (ph + 1))
                    for c in range(4):
                        k = min(P, ACC - P * c)
                        last = T.transpose(W[0][0:k, P * c:P * c + P], X[:, P * c:P * c + k], ident)
                    last.then_inc(s_ntr, 1)
                    pe.wait_ge(s_ntc, ph + 1)
                    for c in range(4):
                        k = min(P, ACC - P * c)
                        r = wdiag[:, ph, :, :].rearrange("p a f -> p (a f)")[0:k, 0:k]
                        last = T.matmul(W[1][:, P * c:P * c + k], xnt[0:k, P * c:P * c + P], r,
                                        start=True, stop=True)
                    last.then_inc(s_root, 1)
                if ph == 3:
                    for k in range(2):
                        pe.wait_ge(s_bnin, k + 1)
                        T.matmul(H[:, 0:F], live, col2[:], start=True, stop=True).then_inc(s_bnout, 1)


def kernel(**a):
    import numpy as np
    import concourse.bacc as bacc
    from concourse import mybir as mb
    from concourse.bass_utils import run_bass_kernel_spmd as run

    a = {k: np.asarray(v) for k, v in a.items()}
    names = [f"L0_gnn_Wn{k}" for k in (1, 2, 3)] + ["L1_gnn_W1"]
    biases = [f"L0_gnn_bn{k}" for k in (1, 2, 3)] + ["L1_gnn_b1", "L1_gnn_b2"]
    roots = [f"L0_gnn_Wr{k}" for k in (1, 2, 3)] + ["L1_gnn_root"]
    lines = [f"L0_gnn_b{k}" for k in (1, 2, 3)] + ["L1_gnn_bias", "L1_gnn_gamma", "L1_gnn_beta"]
    place = np.arange(P)
    consts = np.zeros((P, CW), np.float32)
    consts[:, 0:P] = np.eye(P)
    consts[:BN, P:2 * P] = 1
    consts[:, 2 * P:3 * P] = place[:, None] < place
    consts[:, 3 * P:4 * P] = place
    consts[:, 4 * P:4 * P + NB] = place[:, None] + P * np.arange(NB)
    consts[:, 4 * P + NB:4 * P + NB + 8] = place[:, None] // F == np.arange(8)
    arrays = {
        "x": a["x"],
        "src": a["src"].reshape(LANES, PER),
        "dst": a["dst"].reshape(LANES, PER),
        "dst_n": a["dst"][:N].reshape(NB, BN).T,
        "ea": a["edge_attr_16"].reshape(LANES, PER * F),
        "wcat": np.concatenate([a[k] for k in names], axis=1),
        "bias3": np.concatenate([a[k] for k in biases])[None, :],
        "rows": np.concatenate([a[k] for k in lines])[None, :],
        "wroot": np.stack([a[k] for k in roots], axis=1),
        "w2": a["L1_gnn_W2"],
        "consts": consts,
        "iota_h": np.arange(NB * P, dtype=np.int16)[None, :],
    }
    arrays = {f"in_{k}": np.ascontiguousarray(v) for k, v in arrays.items()}
    nc = bacc.Bacc("TRN2", target_bir_lowering=False, num_devices=1)
    args = [nc.dram_tensor(k, v.shape, mb.dt.from_np(v.dtype), kind="ExternalInput").ap() for k, v in arrays.items()]
    out = nc.dram_tensor("out_x", (N, F), mb.dt.float32, kind="ExternalOutput").ap()
    gnn_kernel(nc, *args, out)
    return run(nc, [arrays], core_ids=[0]).results[0]["out_x"]
```
